# Optimizing a Trainium2 kernel written in Bass

```python
import numpy as np
import jax
import jax.numpy as jnp

def _softmax(x, axis=-1):
    return jax.nn.softmax(x, axis=axis)

def _gelu(x):
    return jax.nn.gelu(x, approximate=True)

def _silu(x):
    return jax.nn.silu(x)

def _sigmoid(x):
    return jax.nn.sigmoid(x)

def _layernorm(x, axis=-1, eps=1e-05):
    m = jnp.mean(x, axis=axis, keepdims=True)
    v = jnp.var(x, axis=axis, keepdims=True)
    return (x - m) / jnp.sqrt(v + eps)

def _scatter_add(tgt, idx, src, axis=0):
    return tgt.at[idx].add(src)

def _segment_sum(src, seg, n):
    return jax.ops.segment_sum(src, seg, n)
kernel_name = 'mk_adj_preln_d2_adj_r2_13609b'

def setup_inputs(seed: int=0):
    np.random.seed(seed)
    _w = jnp.asarray

    def _rec_inputs():
        import jax
        import jax.numpy as jnp
        _gk = jax.random.key(seed)
        x = -6.503e-05 + 0.07158 * jax.random.normal(jax.random.fold_in(_gk, 1), (8192, 128), jnp.float32)
        _w = (1.0 + jnp.arange(8192, dtype=jnp.float32)) ** (-0.5)
        _w = _w / _w.mean()
        _pij = jnp.clip(0.000244141 * _w[:, None] * _w[None, :], 0.0, 1.0)
        _a = jax.random.uniform(jax.random.fold_in(_gk, 2), (8192, 8192)) < _pij
        _a = jnp.logical_or(_a, jnp.eye(8192, dtype=bool))
        _af = _a.astype(jnp.float32)
        _af = _af / jnp.maximum(_af.sum(-1, keepdims=True), 1.0)
        adj = _af
        return (x, adj)
    x, adj = _rec_inputs()

    def _L0_gnn_setup():
        import jax, jax.numpy as jnp
        import numpy as np
        EPS = 1e-05
        MIN_NORM = 1e-15

        def _norm(x):
            return jnp.maximum(jnp.linalg.norm(x, axis=-1, keepdims=True), MIN_NORM)

        def _artanh(x):
            return jnp.arctanh(jnp.clip(x, -1.0 + EPS, 1.0 - EPS))

        def expmap0(u):
            un = _norm(u)
            return jnp.tanh(un) * u / un

        def logmap0(y):
            yn = _norm(y)
            return _artanh(yn) * y / yn

        def mobius_matvec(W, x):
            mx = x @ W
            xn = _norm(x)
            mxn = _norm(mx)
            res = jnp.tanh(mxn / xn * _artanh(xn)) * mx / mxn
            zero = jnp.all(mx == 0.0, axis=-1, keepdims=True)
            return jnp.where(zero, 0.0, res)

        def mobius_scalar_mul(r, x):
            xn = _norm(x)
            return jnp.tanh(r * _artanh(xn)) * x / xn

        def _clamp_abs(x, eps=1e-10):
            return jnp.where(x >= 0.0, jnp.maximum(x, eps), jnp.minimum(x, -eps))
        key = jax.random.key(seed)
        k1, k2, k3 = jax.random.split(key, 3)
        N, D_IN, D_OUT = (4096, 128, 128)
        AVG_DEG = 64.0
        v = 0.1 * jax.random.normal(k1, (N, D_IN), dtype=jnp.float32)
        X = expmap0(v)
        mask = (jax.random.uniform(k2, (N, N)) < AVG_DEG / N).astype(jnp.float32)
        mask = mask + jnp.eye(N, dtype=jnp.float32)
        A_hat = mask / mask.sum(-1, keepdims=True)
        W = jax.random.uniform(k3, (D_IN, D_OUT), dtype=jnp.float32)
        return {'X': X, 'A_hat': A_hat, 'W': W}
    _L0_gnn_all = _L0_gnn_setup()
    _L0_gnn_in = {k: v for k, v in _L0_gnn_all.items() if k in ('W',)}
    del _L0_gnn_all

    def _L1_gnn_setup():
        import jax, jax.numpy as jnp
        import numpy as np
        N = 4096
        D_IN = 128
        D_OUT = 128
        key = jax.random.key(seed)
        k1, k2, k3, k4 = jax.random.split(key, 4)
        x = jax.random.normal(k1, (N, D_IN), dtype=jnp.float32)
        adj = jax.random.uniform(k2, (N, N), dtype=jnp.float32)
        bound = 1.0 / np.sqrt(D_IN)
        W = jax.random.uniform(k3, (D_OUT, D_IN), minval=-bound, maxval=bound, dtype=jnp.float32)
        b = jax.random.uniform(k4, (D_OUT,), minval=-bound, maxval=bound, dtype=jnp.float32)
        return {'x': x, 'adj': adj, 'W': W, 'b': b}
    _L1_gnn_all = _L1_gnn_setup()
    _L1_gnn_in = {k: v for k, v in _L1_gnn_all.items() if k in ('W', 'b')}
    del _L1_gnn_all
    return {'x': x, 'adj': adj, 'L0_gnn_W': _L0_gnn_in['W'], 'L1_gnn_W': _L1_gnn_in['W'], 'L1_gnn_b': _L1_gnn_in['b']}

def reference(x, adj, L0_gnn_W, L1_gnn_W, L1_gnn_b):
    import jax
    import jax.numpy as jnp

    def _L0_gnn_ref(X, A_hat, W):
        import jax, jax.numpy as jnp
        import numpy as np
        EPS = 1e-05
        MIN_NORM = 1e-15

        def _norm(x):
            return jnp.maximum(jnp.linalg.norm(x, axis=-1, keepdims=True), MIN_NORM)

        def _artanh(x):
            return jnp.arctanh(jnp.clip(x, -1.0 + EPS, 1.0 - EPS))

        def expmap0(u):
            un = _norm(u)
            return jnp.tanh(un) * u / un

        def logmap0(y):
            yn = _norm(y)
            return _artanh(yn) * y / yn

        def mobius_matvec(W, x):
            mx = x @ W
            xn = _norm(x)
            mxn = _norm(mx)
            res = jnp.tanh(mxn / xn * _artanh(xn)) * mx / mxn
            zero = jnp.all(mx == 0.0, axis=-1, keepdims=True)
            return jnp.where(zero, 0.0, res)

        def mobius_scalar_mul(r, x):
            xn = _norm(x)
            return jnp.tanh(r * _artanh(xn)) * x / xn

        def _clamp_abs(x, eps=1e-10):
            return jnp.where(x >= 0.0, jnp.maximum(x, eps), jnp.minimum(x, -eps))
        XW = mobius_matvec(W, X)
        sq = jnp.sum(XW * XW, axis=-1, keepdims=True)
        gamma = 2.0 / jnp.maximum(1.0 - sq, EPS)
        nominator = A_hat @ (gamma * XW)
        denominator = _clamp_abs(A_hat @ (gamma - 1.0))
        two_mean = nominator / denominator
        m = mobius_scalar_mul(0.5, two_mean)
        r = A_hat.sum(-1, keepdims=True)
        AXW = mobius_scalar_mul(r, m)
        return expmap0(jax.nn.relu(logmap0(AXW)))

    def _L1_gnn_ref(x, adj, W, b):
        import jax, jax.numpy as jnp
        import numpy as np
        N = 4096
        D_IN = 128
        D_OUT = 128
        rowsum = adj.sum(axis=1)
        d_inv_sqrt = jnp.power(rowsum, -0.5)
        d_inv_sqrt = jnp.where(jnp.isinf(d_inv_sqrt), 0.0, d_inv_sqrt)
        adj_norm = d_inv_sqrt[:, None] * adj * d_inv_sqrt[None, :]
        h = adj_norm @ x
        return h @ W.T + b
    h = jnp.maximum(_layernorm(x, axis=-1), 0.0)
    x = x + _L0_gnn_ref(h, adj, L0_gnn_W)
    h = jnp.maximum(_layernorm(x, axis=-1), 0.0)
    x = x + _L1_gnn_ref(h, adj, L1_gnn_W, L1_gnn_b)
    return x

_drawn_inputs = setup_inputs


def setup_inputs(seed=0):
    import zlib

    import numpy as np

    out = dict(_drawn_inputs(seed))
    spreads = {}
    factors = {}
    for name, (base, spread) in spreads.items():
        noise = np.random.default_rng([zlib.crc32(name.encode()), seed]).standard_normal(out[name].shape)
        drawn = base * np.exp(spread * noise) if base else spread * noise
        out[name] = jnp.asarray(drawn.astype(out[name].dtype))
    for name, factor in factors.items():
        out[name] = (out[name] * factor).astype(out[name].dtype)
    return out
```

```python
from contextlib import ExitStack

import numpy as np

import concourse.bass as bass
from concourse import mybir

F32 = mybir.dt.float32
F32R = mybir.dt.float32r
U32 = mybir.dt.uint32
ALU = mybir.AluOpType
ACT = mybir.ActivationFunctionType

P = 128
D = 128
NT = 64
N = P * NT
Q = 4
G = NT // Q
CJ = NT // Q
CHUNK = Q * Q * P
CHUNKS = G * CJ
PAIRS = G // 2
PC = 2 * CJ
PT = 2 * Q
RAW = 4
HALF = CHUNK // 2
BUF = 4
VW = D + 2
PB = 16
NB = NT // PB
LN_EPS = 1e-5
MIN_NORM = 1e-15
ONE = float(np.float32(1.0 - 1e-5))
CLIP = float(np.arctanh(np.float64(np.float32(ONE))))


def build_program(nc, x, adj, W0, W1T, b1, ident_in, out):
    with ExitStack() as ctx:
        def sb(name, shape, dt=F32):
            return ctx.enter_context(nc.sbuf_tensor(name, shape, dt))

        def sem(name):
            return ctx.enter_context(nc.semaphore(name))

        x_sb = sb("x_sb", [P, NT, D])
        z_sb = sb("z_sb", [P, NT, D])
        v_cat = sb("v_cat", [P, NT, 2 * VW], F32R)
        v_l1 = v_cat[:].rearrange("p t c -> p (t c)")[:, 0:NT * 2 * D].rearrange("p (t c) -> p t c", t=NT)
        raw = sb("raw", [P, RAW, CHUNK])
        hi = sb("hi", [P, BUF, HALF], F32R)
        lo = sb("lo", [P, BUF, HALF], F32R)
        featT = sb("featT", [P, 2, Q * P])
        num_lo = sb("num_lo", [P, Q, VW])
        dr = sb("dr", [P, NT, 2])
        w0_sb = sb("w0_sb", [P, D])
        w1t_sb = sb("w1t_sb", [P, D])
        b_sb = sb("b_sb", [P, D])
        ident = sb("ident", [P, P])
        squares = sb("squares", [P, PT, D], mybir.dt.bfloat16)
        held = sb("held", [P, 1])
        dinv = sb("dinv", [P, NT])
        bn6 = sb("bn6", [P, PB, 6])
        mv = sb("mv", [P, 2, PB, 2])
        rstd = sb("rstd", [P, 2, PB])
        sq2 = sb("sq2", [P, 2, 2, PB])
        cols = sb("cols", [P, 24, 2 * PB])
        num = ctx.enter_context(nc.psum_tensor("num", [P, 8, 512], F32))

        x_landed = [sem(f"x_landed{b}") for b in range(NB)]
        consts_landed = sem("consts_landed")
        slot_landed = [sem(f"slot_landed{s}") for s in range(RAW)]
        hi_ready = sem("hi_ready")
        lo_ready = sem("lo_ready")
        half_used = sem("half_used")
        banks_free = sem("banks_free")
        dve_chain = sem("dve_chain")
        act_chain = sem("act_chain")
        ones_set = sem("ones_set")
        var_ready = sem("var_ready")
        std_ready = sem("std_ready")
        h_ready = sem("h_ready")
        hT_ps = sem("hT_ps")
        hT_ready = sem("hT_ready")
        mx_ready = sem("mx_ready")
        sums_ready = sem("sums_ready")
        norms_ready = sem("norms_ready")
        ln_in = sem("ln_in")
        ln_out = sem("ln_out")
        th_in = sem("th_in")
        th_out = sem("th_out")
        v_ready = sem("v_ready")
        vhi_ready = sem("vhi_ready")
        vlo_ready = sem("vlo_ready")
        numlo_ready = sem("numlo_ready")
        n_norm = sem("n_norm")
        e_ln_in = sem("e_ln_in")
        e_ln_out = sem("e_ln_out")
        u_scale = sem("u_scale")
        u_norm = sem("u_norm")
        e_th_in = sem("e_th_in")
        e_th_out = sem("e_th_out")
        x1_var = sem("x1_var")
        x1_std = sem("x1_std")
        v1_scale = sem("v1_scale")
        v1_ready = sem("v1_ready")
        x1b_ready = sem("x1b_ready")
        v2hi_ready = sem("v2hi_ready")
        v2lo_ready = sem("v2lo_ready")
        agg_ready = sem("agg_ready")
        lin_ready = sem("lin_ready")
        out_ready = sem("out_ready")
        stored = sem("stored")

        x_dram = x.rearrange("(p t) d -> p t d", t=NT)
        out_dram = out.rearrange("(p t) d -> p t d", t=NT)
        block = ctx.enter_context(nc.Block())

        @block.sync
        def _(sp):
            sp.dma_start(x_sb[:, 0:PB, :], x_dram[:, 0:PB, :]).then_inc(x_landed[0], 16)
            for dst, src in ((ident, ident_in), (w0_sb, W0), (w1t_sb, W1T)):
                sp.dma_start(dst[:], src).then_inc(consts_landed, 16)
            sp.dma_start(b_sb[:], b1.rearrange("(o d) -> o d", o=1).to_broadcast([P, D])).then_inc(consts_landed, 16)
            for b in range(1, NB):
                sp.dma_start(x_sb[:, b * PB:(b + 1) * PB, :], x_dram[:, b * PB:(b + 1) * PB, :]).then_inc(x_landed[b], 16)

            def load(c, slot):
                sp.dma_start(raw[:, slot, :], adj[bass.ds(c * P, P), :]).then_inc(slot_landed[slot], 16)

            def store(g):
                sp.wait_ge(out_ready, g + 1)
                sp.dma_start(out_dram[:, bass.ds(g * Q, Q), :], x_sb[:, bass.ds(g * Q, Q), :]).then_inc(stored, 16)

            for s in range(RAW):
                load(s, s)
            with sp.Fori(1, CHUNKS // RAW) as u:
                for s in range(RAW):
                    sp.wait_ge(lo_ready, u * (2 * RAW) + 2 * (s - RAW + 1))
                    load(u * RAW + s, s)

            def pair(p):
                first = isinstance(p, int)
                for k in range(PC):
                    sp.wait_ge(lo_ready, p * (2 * PC) + 2 * (CHUNKS + k - RAW + 1))
                    load(p * PC + k, k % RAW)
                    if k == 10 and not first:
                        store(p * 2 + (-1))
                    if k == 26:
                        store(p * 2)

            pair(0)
            with sp.Fori(1, PAIRS) as p:
                pair(p)
            store(G - 1)
            sp.wait_ge(stored, 16 * G)

        @block.gpsimd
        def _(pool):
            nc.gpsimd.memset(v_cat[:, :, D + 1:D + 2].bitcast(F32), 1.0).then_inc(ones_set, 1)
            nc.gpsimd.memset(v_cat[:, :, VW + D + 1:VW + D + 2].bitcast(F32), 0.0).then_inc(ones_set, 1)
            pool.wait_ge(consts_landed, 64)

            def residual(p):
                pool.wait_ge(v1_ready, p + 1)
                xs = x_sb[:, bass.ds(p * PT, PT), :]
                bias = b_sb[:].rearrange("p (o d) -> p o d", o=1).to_broadcast([P, PT, D])
                nc.gpsimd.tensor_tensor(xs, xs, bias, ALU.add).then_inc(x1b_ready, 1)

            with pool.Fori(0, PAIRS) as p:
                residual(p)

        @block.scalar
        def _(act):
            spare = lo[:].rearrange("p b n -> p (b n)").rearrange("p (s i d) -> p s i d", s=2, i=PB)

            def std(b):
                act.wait_ge(var_ready, b + 1)
                nc.scalar.activation(rstd[:, b % 2, :], rstd[:, b % 2, :], ACT.Sqrt).then_inc(std_ready, 1)

            def h_norms(b):
                act.wait_ge(h_ready, b + 1)
                for i in range(PB):
                    ins = nc.scalar.activation(spare[:, 0, i, :], z_sb[:, b * PB + i, :], ACT.Square,
                                               accum_out=sq2[:, b % 2, 0, i:i + 1])
                ins.then_inc(act_chain, 1)

            def move_hT(b):
                for q in range(b * Q, b * Q + Q):
                    act.wait_ge(hT_ps, q + 1)
                    if q >= 2:
                        act.wait_ge(mx_ready, q - 1)
                    nc.scalar.activation(featT[:, q % 2, :], num[:, 6 + q % 2, :], ACT.Copy).then_inc(hT_ready, 1)

            def mx_norms(b):
                act.wait_ge(mx_ready, b * Q + Q)
                act.wait_ge(act_chain, 2 * b + 1)
                for i in range(PB):
                    q = b * Q + i // Q
                    ins = nc.scalar.activation(spare[:, 1, i, :], num[:, q % 6, (i % Q) * D:(i % Q + 1) * D], ACT.Square,
                                               accum_out=sq2[:, b % 2, 1, i:i + 1])
                ins.then_inc(act_chain, 1)
                act.wait_ge(act_chain, 2 * b + 2)
                nc.scalar.activation(cols[:, 0, :], sq2[:, b % 2, :, :].rearrange("p a b -> p (a b)"), ACT.Sqrt).then_inc(norms_ready, 1)

            for b in range(NB):
                std(b)
                h_norms(b)
                move_hT(b)
                mx_norms(b)
                act.wait_ge(ln_in, b + 1)
                nc.scalar.activation(cols[:, 5, 0:PB], cols[:, 4, 0:PB], ACT.Ln).then_inc(ln_out, 1)
                act.wait_ge(th_in, b + 1)
                nc.scalar.activation(cols[:, 12, 0:PB], cols[:, 11, 0:PB], ACT.Tanh).then_inc(th_out, 1)
                act.wait_ge(v_ready, b + 1)
                act.wait_ge(ones_set, 2)
                nc.scalar.activation(v_cat[:, b * PB:(b + 1) * PB, 0:D], z_sb[:, b * PB:(b + 1) * PB, :], ACT.Copy)
                nc.scalar.activation(v_cat[:, b * PB:(b + 1) * PB, D], cols[:, 15, 0:PB], ACT.Copy).then_inc(vhi_ready, 1)

            chain0 = 2 * NB

            def split_hi(p, k, done):
                c0 = done + k
                act.wait_ge(slot_landed[k % RAW], p * (PC // RAW * 16) + (16 * (c0 // RAW) + 16))
                for h in range(2):
                    n0 = 2 * c0 + h
                    if not (isinstance(p, int) and n0 < BUF):
                        act.wait_ge(half_used, p * (2 * PC) + (n0 - BUF + 1))
                    nc.scalar.activation(hi[:, n0 % BUF, :], raw[:, k % RAW, h * HALF:(h + 1) * HALF], ACT.Copy).then_inc(hi_ready, 1)

            def take_num_lo(g, par):
                act.wait_ge(half_used, g * (2 * CJ) + 2 * CJ)
                act.wait_ge(banks_free, g + 2)
                nc.scalar.activation(num_lo[:], num[:, 4 * par:4 * par + 4, VW:2 * VW], ACT.Copy).then_inc(numlo_ready, 1)

            def tile_norms(t0, base):
                for i in range(PT):
                    ins = nc.scalar.activation(squares[:, i, :], z_sb[:, bass.ds(t0 + i, 1), :].rearrange("p a b -> p (a b)"), ACT.Square,
                                               accum_out=sq2[:, 0, base, i:i + 1])
                return ins

            def wait_holder():
                nc.scalar.activation(held[:], cols[:, 13, 0:1], ACT.Copy)

            def epilogue_step(k, p):
                t0 = p * PT + (-PT)
                if k == 2:
                    take_num_lo(p * 2 + (-1), 1)
                if k == 3:
                    act.wait_ge(banks_free, p * 2 + 2)
                    tile_norms(t0, 0).then_inc(act_chain, 1)
                    act.wait_ge(act_chain, p * 2 + (chain0 - 1))
                    nc.scalar.activation(cols[:, 0, 0:PT], sq2[:, 0, 0, 0:PT], ACT.Sqrt).then_inc(n_norm, 1)
                if k == 5:
                    act.wait_ge(e_ln_in, p)
                    nc.scalar.activation(cols[:, 5, 0:PT], cols[:, 4, 0:PT], ACT.Ln).then_inc(e_ln_out, 1)
                if k == 7:
                    act.wait_ge(u_scale, p)
                    wait_holder()
                    for i in range(PT):
                        zt = z_sb[:, bass.ds(t0 + i, 1), :].rearrange("p a b -> p (a b)")
                        ins = nc.scalar.activation(zt, zt, ACT.Relu, scale=cols[:, 13, i:i + 1])
                    ins.then_inc(act_chain, 1)
                if k == 8:
                    act.wait_ge(act_chain, p * 2 + chain0)
                    wait_holder()
                    tile_norms(t0, 1).then_inc(u_norm, 1)
                    act.wait_ge(u_norm, p * 2 + (-1))
                    nc.scalar.activation(cols[:, 0, 0:PT], sq2[:, 0, 1, 0:PT], ACT.Sqrt).then_inc(u_norm, 1)
                if k == 9:
                    act.wait_ge(e_th_in, p)
                    nc.scalar.activation(cols[:, 12, 0:PT], cols[:, 11, 0:PT], ACT.Tanh).then_inc(e_th_out, 1)
                if k == 11:
                    act.wait_ge(x1_var, p)
                    nc.scalar.activation(cols[:, 16, 0:2 * PT], cols[:, 16, 0:2 * PT], ACT.Sqrt).then_inc(x1_std, 1)
                if k == 12:
                    act.wait_ge(v1_scale, p)
                    wait_holder()
                    for i in range(PT):
                        zt = z_sb[:, bass.ds(t0 + i, 1), :].rearrange("p a b -> p (a b)")
                        xt = x_sb[:, bass.ds(t0 + i, 1), :].rearrange("p a b -> p (a b)")
                        ins = nc.scalar.activation(zt, xt, ACT.Relu, scale=cols[:, 18, i:i + 1], bias=cols[:, 19, i:i + 1])
                    ins.then_inc(v1_ready, 1)

            def pair0(p):
                first = isinstance(p, int)
                for k in range(PC):
                    split_hi(p, k, 0)
                    if not first:
                        epilogue_step(k, p)
                    if k == CJ + 2:
                        take_num_lo(p * 2, 0)

            pair0(0)
            with act.Fori(1, PAIRS) as p:
                pair0(p)

            def split_v_hi(b):
                act.wait_ge(half_used, 2 * CHUNKS)
                act.wait_ge(v1_ready, 2 * b + 2)
                nc.scalar.activation(v_l1[:, b * PB:(b + 1) * PB, 0:D], z_sb[:, b * PB:(b + 1) * PB, :], ACT.Copy).then_inc(v2hi_ready, 1)

            def take_agg(g, par):
                act.wait_ge(half_used, g * (2 * CJ) + 2 * (CHUNKS + CJ))
                if not (isinstance(g, int) and g < 1):
                    act.wait_ge(lin_ready, g)
                nc.scalar.activation(featT[:, par, :], num[:, par, :], ACT.Copy).then_inc(agg_ready, 1)

            def pair1(p):
                first = isinstance(p, int)
                for k in range(PC):
                    split_hi(p, k, CHUNKS)
                    if first:
                        epilogue_step(k, PAIRS)
                        if k < CJ and k % Q == 1:
                            split_v_hi(k // Q)
                    elif k == 2:
                        take_agg(p * 2 + (-1), 1)
                    if k == CJ + 2:
                        take_agg(p * 2, 0)

            pair1(0)
            with act.Fori(1, PAIRS) as p:
                pair1(p)
            take_agg(G - 1, 1)

        @block.vector
        def _(dve):
            count = [0]

            def link(ins, base=0):
                count[0] += 1
                ins.then_inc(dve_chain, 1)
                dve.wait_ge(dve_chain, base + count[0])

            V = nc.vector

            def artanh_before_ln(z, n, base):
                link(V.tensor_scalar(cols[:, 2, 0:n], z, -1.0, 1.0, ALU.mult, ALU.add), base)
                link(V.reciprocal(cols[:, 3, 0:n], cols[:, 2, 0:n]), base)
                return V.scalar_tensor_tensor(out=cols[:, 4, 0:n], in0=z, scalar=1.0, in1=cols[:, 3, 0:n],
                                              op0=ALU.add, op1=ALU.mult)

            def artanh_series(z, n, base):
                w, s = cols[:, 6, 0:n], cols[:, 7, 0:n]
                V.tensor_scalar(cols[:, 8, 0:n], z, 0.1, None, ALU.is_lt)
                link(V.tensor_tensor(w, z, z, ALU.mult), base)
                link(V.tensor_scalar(s, w, 1.0 / 9, None, ALU.mult), base)
                for c in (1.0 / 7, 1.0 / 5, 1.0 / 3):
                    link(V.scalar_tensor_tensor(out=s, in0=s, scalar=c, in1=w, op0=ALU.add, op1=ALU.mult), base)
                link(V.scalar_tensor_tensor(out=s, in0=s, scalar=1.0, in1=z, op0=ALU.add, op1=ALU.mult), base)

            def artanh_after_ln(n, base, between=lambda: None):
                a = cols[:, 9, 0:n]
                link(V.tensor_scalar(a, cols[:, 5, 0:n], 0.5, None, ALU.mult), base)
                between()
                link(V.copy_predicated(a, cols[:, 8, 0:n].bitcast(U32), cols[:, 7, 0:n]), base)
                return a

            def stats(b):
                dve.wait_ge(x_landed[b], 16)
                for i in range(PB):
                    ins = V.bn_stats(bn6[:, i, :], x_sb[:, b * PB + i, :])
                link(ins)
                for i in range(PB):
                    ins = V.bn_aggr(mv[:, b % 2, i, :], bn6[:, i, :])
                link(ins)
                V.tensor_scalar(rstd[:, b % 2, :], mv[:, b % 2, :, 1], LN_EPS, None, ALU.add).then_inc(var_ready, 1)

            def h_of(b):
                dve.wait_ge(std_ready, b + 1)
                link(V.reciprocal(rstd[:, b % 2, :], rstd[:, b % 2, :]))
                for i in range(PB):
                    ins = V.tensor_scalar(z_sb[:, b * PB + i, :], x_sb[:, b * PB + i, :], mv[:, b % 2, i, 0:1],
                                          rstd[:, b % 2, i:i + 1], ALU.subtract, ALU.mult)
                link(ins)
                zb = z_sb[:, b * PB:(b + 1) * PB, :]
                V.tensor_scalar(zb, zb, 0.0, None, ALU.max).then_inc(h_ready, 1)

            def operand(b):
                n = PB
                dve.wait_ge(norms_ready, b + 1)
                norms = cols[:, 1, :]
                link(V.tensor_scalar(norms, cols[:, 0, :], MIN_NORM, None, ALU.max))
                z = cols[:, 10, 0:n]
                link(V.tensor_scalar(z, norms[:, 0:n], ONE, None, ALU.min))
                artanh_before_ln(z, n, 0).then_inc(ln_in, 1)
                artanh_series(z, n, 0)
                rn = cols[:, 14, :]
                link(V.reciprocal(rn, norms))
                w = cols[:, 11, 0:n]
                link(V.tensor_tensor(w, norms[:, n:2 * n], rn[:, 0:n], ALU.mult))
                dve.wait_ge(ln_out, b + 1)
                a = artanh_after_ln(n, 0)
                V.tensor_tensor(w, w, a, ALU.mult).then_inc(th_in, 1)
                dve.wait_ge(th_out, b + 1)
                c, s, gm = cols[:, 13, 0:n], cols[:, 16, 0:n], cols[:, 17, 0:n]
                link(V.tensor_tensor(c, cols[:, 12, 0:n], rn[:, n:2 * n], ALU.mult))
                link(V.tensor_tensor(s, c, cols[:, 0, n:2 * n], ALU.mult))
                link(V.tensor_tensor(s, s, s, ALU.mult))
                link(V.tensor_scalar(s, s, -1.0, 1.0, ALU.mult, ALU.add))
                link(V.tensor_scalar(s, s, LN_EPS, None, ALU.max))
                link(V.reciprocal(gm, s))
                link(V.scalar_tensor_tensor(out=c, in0=gm, scalar=2.0, in1=c, op0=ALU.mult, op1=ALU.mult))
                V.tensor_scalar(cols[:, 15, 0:n], gm, 2.0, -1.0, ALU.mult, ALU.add)
                for i in range(Q):
                    q = b * Q + i
                    zq = z_sb[:, q * Q:(q + 1) * Q, :]
                    mx = num[:, q % 6, :].rearrange("p (a b) -> p a b", a=Q)
                    cb = cols[:, 13, i * Q:(i + 1) * Q].rearrange("p (a o) -> p a o", o=1).to_broadcast([P, Q, D])
                    ins = V.tensor_tensor(zq, mx, cb, ALU.mult)
                ins.then_inc(v_ready, 1)
                dve.wait_ge(vhi_ready, b + 1)
                vb = v_cat[:, b * PB:(b + 1) * PB, :]
                V.tensor_tensor(vb[:, :, VW:VW + D], z_sb[:, b * PB:(b + 1) * PB, :], vb[:, :, 0:D].bitcast(F32), ALU.subtract)
                V.tensor_tensor(vb[:, :, VW + D], cols[:, 15, 0:n], vb[:, :, D].bitcast(F32), ALU.subtract).then_inc(vlo_ready, 1)

            stats(0)
            h_of(0)
            for b in range(NB):
                if b + 1 < NB:
                    stats(b + 1)
                operand(b)
                if b + 1 < NB:
                    h_of(b + 1)
            dve.wait_ge(vlo_ready, NB)
            V.memset(cols[:, 20, 0:1], 0.0).then_inc(banks_free, 2)
            chain0 = count[0]

            def split_lo(p, k, done):
                for h in range(2):
                    n0 = 2 * (done + k) + h
                    dve.wait_ge(hi_ready, p * (2 * PC) + (n0 + 1))
                    V.tensor_tensor(lo[:, n0 % BUF, :], raw[:, k % RAW, h * HALF:(h + 1) * HALF],
                                    hi[:, n0 % BUF, :].bitcast(F32), ALU.subtract).then_inc(lo_ready, 1)

            def take_num(g, par):
                dve.wait_ge(numlo_ready, g + 1)
                bank = num[:, 4 * par:4 * par + 4, :]
                V.tensor_tensor(z_sb[:, bass.ds(g * Q, Q), :], bank[:, :, 0:D], num_lo[:, :, 0:D], ALU.add)
                V.tensor_tensor(dr[:, bass.ds(g * Q, Q), :], bank[:, :, D:VW], num_lo[:, :, D:VW], ALU.add).then_inc(banks_free, 1)

            LINKS = 31

            def epilogue_step(k, p):
                n = PT
                base = p * LINKS + (chain0 - LINKS)
                t0 = p * PT + (-PT)
                den = dr[:, bass.ds(t0, n), 0:1].rearrange("p a b -> p (a b)")
                r = dr[:, bass.ds(t0, n), 1:2].rearrange("p a b -> p (a b)")
                z, tn, inv, w = cols[:, 10, 0:n], cols[:, 1, 0:n], cols[:, 14, 0:n], cols[:, 11, 0:n]
                if k == 2:
                    count[0] = 0
                    take_num(p * 2 + (-1), 1)
                if k == 3:
                    dve.wait_ge(banks_free, p * 2 + 2)
                    ge, lt = cols[:, 15, 0:n], cols[:, 16, 0:n]
                    V.tensor_scalar(ge, den, 0.0, None, ALU.is_ge)
                    link(V.tensor_scalar(lt, den, 0.0, None, ALU.is_lt), base)
                    V.scalar_tensor_tensor(out=ge, in0=den, scalar=1e-10, in1=ge, op0=ALU.max, op1=ALU.mult)
                    link(V.scalar_tensor_tensor(out=lt, in0=den, scalar=-1e-10, in1=lt, op0=ALU.min, op1=ALU.mult), base)
                    link(V.tensor_tensor(inv, ge, lt, ALU.add), base)
                    link(V.reciprocal(inv, inv), base)
                if k == 4:
                    dve.wait_ge(n_norm, p)
                    link(V.scalar_tensor_tensor(out=tn, in0=inv, scalar=-1.0, in1=inv, op0=ALU.mult, op1=ALU.max), base)
                    link(V.tensor_tensor(tn, tn, cols[:, 0, 0:n], ALU.mult), base)
                    link(V.tensor_scalar(tn, tn, MIN_NORM, None, ALU.max), base)
                    link(V.tensor_scalar(z, tn, ONE, None, ALU.min), base)
                    artanh_before_ln(z, n, base).then_inc(e_ln_in, 1)
                if k == 5:
                    artanh_series(z, n, base)
                    link(V.reciprocal(tn, tn), base)
                    link(V.tensor_tensor(inv, inv, tn, ALU.mult), base)
                if k == 6:
                    dve.wait_ge(e_ln_out, p)
                    a = artanh_after_ln(n, base, lambda: V.tensor_scalar(w, r, 0.5, None, ALU.mult))
                    link(V.tensor_tensor(w, w, a, ALU.mult), base)
                    link(V.tensor_scalar(w, w, CLIP, -CLIP, ALU.min, ALU.max), base)
                    V.tensor_tensor(cols[:, 13, 0:n], w, inv, ALU.mult).then_inc(u_scale, 1)
                if k == 8:
                    dve.wait_ge(u_norm, p * 2)
                    V.tensor_scalar(w, cols[:, 0, 0:n], MIN_NORM, None, ALU.max).then_inc(e_th_in, 1)
                if k == 9:
                    dve.wait_ge(e_th_in, p)
                    link(V.reciprocal(cols[:, 15, 0:n], w), base)
                    dve.wait_ge(e_th_out, p)
                    link(V.tensor_tensor(cols[:, 15, 0:n], cols[:, 15, 0:n], cols[:, 12, 0:n], ALU.mult), base)
                    for i in range(n):
                        xt = x_sb[:, bass.ds(t0 + i, 1), :].rearrange("p a b -> p (a b)")
                        zt = z_sb[:, bass.ds(t0 + i, 1), :].rearrange("p a b -> p (a b)")
                        ins = V.scalar_tensor_tensor(out=xt, in0=zt, scalar=cols[:, 15, i:i + 1], in1=xt, op0=ALU.mult, op1=ALU.add)
                    link(ins, base)
                if k == 10:
                    for i in range(n):
                        ins = V.bn_stats(bn6[:, i, :], x_sb[:, bass.ds(t0 + i, 1), :].rearrange("p a b -> p (a b)"))
                    link(ins, base)
                    zero = cols[:, 15, 0:n]
                    V.tensor_scalar(zero, r, 0.0, None, ALU.is_equal)
                    for i in range(n):
                        ins = V.bn_aggr(mv[:, 0, i, :], bn6[:, i, :])
                    link(ins, base)
                    V.tensor_scalar(cols[:, 16, 0:n], mv[:, 0, 0:n, 1], LN_EPS, None, ALU.add)
                    link(V.tensor_tensor(cols[:, 16, n:2 * n], r, zero, ALU.add), base)
                    V.tensor_scalar(cols[:, 17, 0:n], zero, -1.0, 1.0, ALU.mult, ALU.add).then_inc(x1_var, 1)
                if k == 11:
                    dve.wait_ge(x1_std, p)
                    link(V.reciprocal(cols[:, 16, 0:2 * n], cols[:, 16, 0:2 * n]), base)
                    dt = dinv[:, bass.ds(t0, n)]
                    link(V.tensor_tensor(dt, cols[:, 16, n:2 * n], cols[:, 17, 0:n], ALU.mult), base)
                    link(V.tensor_tensor(cols[:, 18, 0:n], cols[:, 16, 0:n], dt, ALU.mult), base)
                    V.scalar_tensor_tensor(out=cols[:, 19, 0:n], in0=mv[:, 0, 0:n, 0], scalar=-1.0, in1=cols[:, 18, 0:n],
                                           op0=ALU.mult, op1=ALU.mult).then_inc(v1_scale, 1)
                    assert count[0] == LINKS

            def pair0(p):
                first = isinstance(p, int)
                for k in range(PC):
                    split_lo(p, k, 0)
                    if not first:
                        epilogue_step(k, p)
                    if k == CJ + 2:
                        take_num(p * 2, 0)

            pair0(0)
            with dve.Fori(1, PAIRS) as p:
                pair0(p)

            def split_v_lo(b):
                dve.wait_ge(v2hi_ready, b + 1)
                vb = v_l1[:, b * PB:(b + 1) * PB, :]
                V.tensor_tensor(vb[:, :, D:2 * D], z_sb[:, b * PB:(b + 1) * PB, :], vb[:, :, 0:D].bitcast(F32), ALU.subtract).then_inc(v2lo_ready, 1)

            def output(g, par):
                dve.wait_ge(lin_ready, g + 1)
                for q in range(Q):
                    xt = x_sb[:, bass.ds(g * Q + q, 1), :].rearrange("p a b -> p (a b)")
                    ins = V.scalar_tensor_tensor(out=xt, in0=num[:, 2 + par, q * D:(q + 1) * D], scalar=dinv[:, bass.ds(g * Q + q, 1)],
                                                 in1=xt, op0=ALU.mult, op1=ALU.add)
                ins.then_inc(out_ready, 1)

            def pair1(p):
                first = isinstance(p, int)
                for k in range(PC):
                    split_lo(p, k, CHUNKS)
                    if first:
                        epilogue_step(k, PAIRS)
                        if k < CJ and k % Q == 1:
                            split_v_lo(k // Q)
                        if k == CJ:
                            dve.wait_ge(x1b_ready, PAIRS)
                    elif k == 4:
                        output(p * 2 + (-1), 1)
                    if k == CJ + 4:
                        output(p * 2, 0)

            pair1(0)
            with dve.Fori(1, PAIRS) as p:
                pair1(p)
            output(G - 1, 1)

        @block.tensor
        def _(pe):
            pe.wait_ge(consts_landed, 64)
            for q in range(G):
                b = q // Q
                pe.wait_ge(h_ready, b + 1)
                if q >= 2:
                    pe.wait_ge(hT_ready, q - 1)
                for i in range(Q):
                    ins = nc.tensor.transpose(num[:, 6 + q % 2, i * P:(i + 1) * P], z_sb[:, q * Q + i, :], ident[:])
                ins.then_inc(hT_ps, 1)
                pe.wait_ge(hT_ready, q + 1)
                if q >= 6:
                    pe.wait_ge(v_ready, (q - 6) // Q + 1)
                for i in range(Q):
                    ins = nc.tensor.matmul(num[:, q % 6, i * D:(i + 1) * D], featT[:, q % 2, i * P:(i + 1) * P], w0_sb[:], start=True, stop=True)
                ins.then_inc(mx_ready, 1)
            pe.wait_ge(vlo_ready, NB)

            def chunk0(par, s, quad, value, first, last):
                for h in range(2):
                    pe.wait_ge(lo_ready, value + h)
                    buf = 2 * s + h
                    for j in range(2):
                        v = v_cat[:, bass.ds(quad * Q + (2 * h + j), 1), :].rearrange("p a b -> p (a b)")
                        for q in range(Q):
                            at = slice((j * Q + q) * P, (j * Q + q + 1) * P)
                            nc.tensor.matmul(num[:, 4 * par + q, 0:2 * VW], hi[:, buf, at], v, start=first and h + j == 0, stop=False, skip_group_check=True)
                            ins = nc.tensor.matmul(num[:, 4 * par + q, 0:VW], lo[:, buf, at], v[:, 0:VW], start=False, stop=last and h + j == 2, skip_group_check=True)
                    ins.then_inc(half_used, 1)

            with pe.Fori(0, PAIRS) as p:
                for par in range(2):
                    pe.wait_ge(banks_free, p * 2 + (par + 1))
                    for s in range(2):
                        chunk0(par, s, s, p * (2 * PC) + (2 * (par * CJ + s) + 1), s == 0, False)
                    with pe.Fori(1, CJ // 2) as u:
                        for s in range(2):
                            chunk0(par, s, u * 2 + s, p * (2 * PC) + u * 4 + (2 * (par * CJ + s) + 1), False, False)

            def linear(g, par):
                pe.wait_ge(agg_ready, g + 1)
                if not (isinstance(g, int) and g < 1):
                    pe.wait_ge(out_ready, g)
                for q in range(Q):
                    ins = nc.tensor.matmul(num[:, 2 + par, q * D:(q + 1) * D], featT[:, par, q * P:(q + 1) * P], w1t_sb[:], start=True, stop=True)
                ins.then_inc(lin_ready, 1)

            def pair1(p):
                first = isinstance(p, int)
                for par in range(2):
                    if first:
                        pe.wait_ge(banks_free, G + 1)
                    else:
                        pe.wait_ge(agg_ready, p * 2 + (par - 1))
                    for k in range(CJ):
                        if first and par == 0 and k % Q == 0:
                            pe.wait_ge(v2lo_ready, k // Q + 1)
                        acc = num[:, par, :]
                        for h in range(2):
                            n0 = 2 * (CHUNKS + par * CJ + k) + h
                            pe.wait_ge(lo_ready, p * (2 * PC) + (n0 + 1))
                            for j in range(2):
                                v = v_l1[:, k * Q + 2 * h + j, :]
                                at = slice(j * Q * P, (j + 1) * Q * P)
                                nc.tensor.matmul(acc, v[:, 0:D], hi[:, n0 % BUF, at], start=k + h + j == 0, stop=False, skip_group_check=True)
                                nc.tensor.matmul(acc, v[:, 0:D], lo[:, n0 % BUF, at], start=False, stop=False, skip_group_check=True)
                                ins = nc.tensor.matmul(acc, v[:, D:2 * D], hi[:, n0 % BUF, at], start=False, stop=k == CJ - 1 and h + j == 2, skip_group_check=True)
                            ins.then_inc(half_used, 1)
                        if k == 3 and not (first and par == 0):
                            linear(p * 2 + (par - 1), 1 - par)

            pair1(0)
            with pe.Fori(1, PAIRS) as p:
                pair1(p)
            linear(G - 1, 1)


def kernel(x, adj, L0_gnn_W, L1_gnn_W, L1_gnn_b):
    import concourse.bacc as _bacc
    from concourse.bass_utils import run_bass_kernel_spmd as _run

    a = np.asarray(adj).reshape(P, G, Q, P, CJ, Q).transpose(1, 4, 3, 5, 2, 0)
    arrays = {
        "x": np.ascontiguousarray(x),
        "adj": np.ascontiguousarray(a).reshape(CHUNKS * P, CHUNK),
        "W0": np.ascontiguousarray(L0_gnn_W),
        "W1T": np.ascontiguousarray(np.asarray(L1_gnn_W).T),
        "b1": np.ascontiguousarray(L1_gnn_b),
        "identity": np.eye(P, dtype=np.float32),
    }
    nc = _bacc.Bacc("TRN2", target_bir_lowering=False, num_devices=1)
    args = [nc.dram_tensor(n, v.shape, mybir.dt.from_np(v.dtype), kind="ExternalInput").ap() for n, v in arrays.items()]
    args.append(nc.dram_tensor("out", (N, D), F32, kind="ExternalOutput").ap())
    build_program(nc, *args)
    r = _run(nc, [arrays], core_ids=[0])
    return r.results[0]["out"]
```

```python
from contextlib import ExitStack

import numpy as np

import concourse.bass as bass
from concourse import mybir

F32 = mybir.dt.float32
F32R = mybir.dt.float32r
BF16 = mybir.dt.bfloat16
U32 = mybir.dt.uint32
ALU = mybir.AluOpType
ACT = mybir.ActivationFunctionType

P = 128
D = 128
NT = 64
N = P * NT
Q = 4
G = NT // Q
CJ = NT // Q
CHUNK = Q * Q * P
CHUNKS = G * CJ
PAIRS = G // 2
PC = 2 * CJ
RING = 8
HALF = CHUNK // 2
BUF = 4
VW = D + 2
FIRST = 3
FIRST_CHUNKS = FIRST * CJ
BATCHES = [(0, 4), (4, 4), (8, 8), (16, 12), (28, 12), (40, 12), (52, 12)]
NB = len(BATCHES)
MB = 12
LN_EPS = 1e-5
MIN_NORM = 1e-15
ONE = float(np.float32(1.0 - 1e-5))
CLIP = float(np.arctanh(np.float64(ONE)))


def first_col(g):
    return g * VW if isinstance(g, int) and g < FIRST else 0


def rotated(k):
    return (k + CJ - RING) % CJ


def group_of(s):
    return G - 1 if isinstance(s, int) and s == 0 else s + (-1)


def last_reader(end):
    quad = (end - 1) // (Q * VW * 4)
    return CHUNKS - RING + quad + 1


def flat(ap):
    return ap.rearrange("p a b -> p (a b)")


def build_program(nc, x, adj, W0, W1T, b1, identity, out):
    with ExitStack() as ctx:
        def sb(name, shape, dt=F32):
            return ctx.enter_context(nc.sbuf_tensor(name, shape, dt))

        def sem(name):
            return ctx.enter_context(nc.semaphore(name))

        x_sb = sb("x_sb", [P, NT, D])
        v_l1 = sb("v_l1", [P, NT, 2 * D], F32R)
        ring = sb("ring", [P, RING, CHUNK])
        featT = sb("featT", [P, 2, Q * P])
        uv = sb("uv", [P, 2 * Q, D])
        u_sb, v_sb = uv[:, 0:Q, :], uv[:, Q:2 * Q, :]
        squares = uv[:].bitcast(BF16).rearrange("p a (b d) -> p (a b) d", b=2)
        held = sb("held", [P, 1])
        w0_sb = sb("w0_sb", [P, D])
        w1t_sb = sb("w1t_sb", [P, D])
        b_sb = sb("b_sb", [P, D])
        ident = sb("ident", [P, P])
        dinv = sb("dinv", [P, NT])
        bn6 = sb("bn6", [P, MB, 6])
        mv = sb("mv", [P, 2, MB, 2])
        rstd = sb("rstd", [P, 2, MB])
        sq2 = sb("sq2", [P, 2, 2, MB])
        cols = sb("cols", [P, 22, 2 * MB])
        with nc.sbuf_tensor("v_l0", [P, NT, VW], F32) as v_l0:
            pass
        lo = sb("lo", [P, BUF, HALF], F32R)
        sb("between", [P, NT // 2 * VW - BUF * HALF])
        hi = sb("hi", [P, BUF, HALF], F32R)
        num = ctx.enter_context(nc.psum_tensor("num", [P, 8, 512], F32))

        x_landed = [sem(f"x_landed{b}") for b in range(NB)]
        consts_landed = sem("consts_landed")
        slot_landed = [sem(f"slot_landed{s}") for s in range(RING)]
        chunk_used = sem("chunk_used")
        half_used = sem("half_used")
        hi_ready = sem("hi_ready")
        lo_ready = sem("lo_ready")
        num_free = sem("num_free")
        dve_chain = sem("dve_chain")
        act_chain = sem("act_chain")
        ones_set = sem("ones_set")
        var_ready = sem("var_ready")
        std_ready = sem("std_ready")
        h_ready = sem("h_ready")
        hT_ps = sem("hT_ps")
        hT_ready = sem("hT_ready")
        mx_ps = sem("mx_ps")
        mx_moved = sem("mx_moved")
        norms_ready = sem("norms_ready")
        ln_in = sem("ln_in")
        ln_out = sem("ln_out")
        th_in = sem("th_in")
        th_out = sem("th_out")
        v0_ready = sem("v0_ready")
        sums_taken = sem("sums_taken")
        n_norm = sem("n_norm")
        e_ln_in = sem("e_ln_in")
        e_ln_out = sem("e_ln_out")
        u_scale = sem("u_scale")
        u_norm = sem("u_norm")
        e_th_in = sem("e_th_in")
        e_th_out = sem("e_th_out")
        x1_var = sem("x1_var")
        x1_std = sem("x1_std")
        v1_scale = sem("v1_scale")
        v1hi_ready = sem("v1hi_ready")
        v1lo_ready = sem("v1lo_ready")
        x1b_ready = sem("x1b_ready")
        agg_ready = sem("agg_ready")
        lin_ready = sem("lin_ready")
        out_ready = sem("out_ready")
        stored = sem("stored")

        x_dram = x.rearrange("(p t) d -> p t d", t=NT)
        out_dram = out.rearrange("(p t) d -> p t d", t=NT)
        block = ctx.enter_context(nc.Block())

        @block.sync
        def _(sp):
            for b, (t0, n) in enumerate(BATCHES):
                sp.dma_start(x_sb[:, t0:t0 + n, :], x_dram[:, t0:t0 + n, :]).then_inc(x_landed[b], 16)
                if b == 0:
                    for dst, src in ((ident, identity), (w0_sb, W0), (w1t_sb, W1T)):
                        sp.dma_start(dst[:], src).then_inc(consts_landed, 16)
                    sp.dma_start(b_sb[:], b1.rearrange("(o d) -> o d", o=1).to_broadcast([P, D])).then_inc(consts_landed, 16)

            def load(c, slot):
                sp.dma_start(ring[:, slot, :], adj[bass.ds(c * P, P), :]).then_inc(slot_landed[slot], 16)

            def store(s):
                g = group_of(s)
                sp.wait_ge(out_ready, s + 1)
                sp.dma_start(out_dram[:, bass.ds(g * Q, Q), :], x_sb[:, bass.ds(g * Q, Q), :]).then_inc(stored, 16)

            for c in range(FIRST_CHUNKS):
                if c >= RING:
                    sp.wait_ge(chunk_used, c - RING + 1)
                load(c % FIRST * CJ + c // FIRST, c % RING)
            with sp.Fori(FIRST, G) as g:
                for k in range(CJ):
                    sp.wait_ge(chunk_used, g * CJ + (k - RING + 1))
                    load(g * CJ + rotated(k), k % RING)

            def pair(p):
                first = isinstance(p, int)
                for k in range(RING if first else 0, PC):
                    sp.wait_ge(lo_ready, p * (2 * PC) + 2 * (k - RING + 1))
                    if first:
                        load((CHUNKS - CJ + k) % CHUNKS, k % RING)
                    else:
                        load(p * PC + (k - CJ), k % RING)
                    if k == 10 and not first:
                        store(p * 2 + (-1))
                    if k == 26:
                        store(p * 2)

            pair(0)
            with sp.Fori(1, PAIRS) as p:
                pair(p)
            store(G - 1)
            sp.wait_ge(stored, 16 * G)

        @block.gpsimd
        def _(pool):
            nc.gpsimd.memset(v_l0[:, :, D + 1:VW], 1.0).then_inc(ones_set, 1)
            pool.wait_ge(consts_landed, 64)

            with pool.Fori(0, G) as g:
                pool.wait_ge(v1hi_ready, g + 1)
                xs = x_sb[:, bass.ds(g * Q, Q), :]
                bias = b_sb[:].rearrange("p (o d) -> p o d", o=1).to_broadcast([P, Q, D])
                nc.gpsimd.tensor_tensor(xs, xs, bias, ALU.add).then_inc(x1b_ready, 1)

        @block.scalar
        def _(act):
            S = nc.scalar
            count = [0]

            def link(ins, base=0):
                count[0] += 1
                ins.then_inc(act_chain, 1)
                act.wait_ge(act_chain, base + count[0])

            def std(b):
                n = BATCHES[b][1]
                act.wait_ge(var_ready, b + 1)
                S.activation(rstd[:, b % 2, 0:n], rstd[:, b % 2, 0:n], ACT.Sqrt).then_inc(std_ready, 1)

            def h_norms(b):
                t0, n = BATCHES[b]
                act.wait_ge(h_ready, b + 1)
                for i in range(n):
                    ins = S.activation(squares[:, i, :], v_l0[:, t0 + i, 0:D], ACT.Square, accum_out=sq2[:, b % 2, 0, i:i + 1])
                link(ins)

            def move_quads(b):
                t0, n = BATCHES[b]
                q0, q1 = t0 // Q, (t0 + n) // Q
                for q in range(q0, q1 + 1):
                    if q < q1:
                        act.wait_ge(hT_ps, q + 1)
                        if q >= 2:
                            act.wait_ge(mx_ps, q - 1)
                        S.activation(featT[:, q % 2, :], num[:, 4 + q % 2, :], ACT.Copy).then_inc(hT_ready, 1)
                    if q > q0:
                        m = q - 1
                        act.wait_ge(mx_ps, m + 1)
                        S.activation(v_l0[:, m * Q:(m + 1) * Q, 0:D], num[:, 6 + m % 2, :].rearrange("p (a d) -> p a d", a=Q), ACT.Copy).then_inc(mx_moved, 1)

            def mx_norms(b):
                t0, n = BATCHES[b]
                act.wait_ge(mx_moved, (t0 + n) // Q)
                for i in range(n):
                    ins = S.activation(squares[:, i, :], v_l0[:, t0 + i, 0:D], ACT.Square, accum_out=sq2[:, b % 2, 1, i:i + 1])
                link(ins)
                if b >= 1:
                    act.wait_ge(v0_ready, b)
                both = cols[:, 0, :].rearrange("p (a n) -> p a n", a=2)[:, :, 0:n]
                S.activation(both, sq2[:, b % 2, :, 0:n], ACT.Sqrt).then_inc(norms_ready, 1)

            std(0)
            h_norms(0)
            std(1)
            move_quads(0)
            for b in range(NB):
                n = BATCHES[b][1]
                mx_norms(b)
                act.wait_ge(ln_in, b + 1)
                S.activation(cols[:, 5, 0:n], cols[:, 4, 0:n], ACT.Ln).then_inc(ln_out, 1)
                if b + 1 < NB:
                    h_norms(b + 1)
                act.wait_ge(th_in, b + 1)
                S.activation(cols[:, 12, 0:n], cols[:, 11, 0:n], ACT.Tanh).then_inc(th_out, 1)
                if b + 1 < NB:
                    move_quads(b + 1)
                if b + 2 < NB:
                    std(b + 2)

            chain0 = count[0]
            LINKS = 3

            def wait_holder():
                S.activation(held[:], cols[:, 13, 0:1], ACT.Copy)

            def epilogue_step(step, g, par):
                base = g * LINKS + chain0
                if step == 0:
                    count[0] = 0
                    if not (isinstance(g, int) and g < 1):
                        act.wait_ge(v1lo_ready, g)
                    act.wait_ge(sums_taken, g + 1)
                    for i in range(Q):
                        ins = S.activation(squares[:, 2 * Q + i, :], num[:, 4 * par + i, first_col(g):first_col(g) + D], ACT.Square, accum_out=sq2[:, 0, 0, i:i + 1])
                    link(ins, base)
                    S.activation(cols[:, 0, 0:Q], sq2[:, 0, 0, 0:Q], ACT.Sqrt).then_inc(n_norm, 1)
                if step == 1:
                    act.wait_ge(e_ln_in, g + 1)
                    S.activation(cols[:, 5, 0:Q], cols[:, 4, 0:Q], ACT.Ln).then_inc(e_ln_out, 1)
                if step == 2:
                    act.wait_ge(u_scale, g + 1)
                    for i in range(Q):
                        ins = S.activation(u_sb[:, i, :], num[:, 4 * par + i, first_col(g):first_col(g) + D], ACT.Relu, scale=cols[:, 13, i:i + 1])
                    ins.then_inc(num_free, 1)
                    act.wait_ge(num_free, g + 2)
                    for i in range(Q):
                        ins = S.activation(squares[:, 3 * Q + i, :], u_sb[:, i, :], ACT.Square, accum_out=sq2[:, 0, 1, i:i + 1])
                    link(ins, base)
                    S.activation(cols[:, 0, 0:Q], sq2[:, 0, 1, 0:Q], ACT.Sqrt).then_inc(u_norm, 1)
                if step == 3:
                    act.wait_ge(e_th_in, g + 1)
                    S.activation(cols[:, 12, 0:Q], cols[:, 11, 0:Q], ACT.Tanh).then_inc(e_th_out, 1)
                if step == 4:
                    act.wait_ge(x1_var, g + 1)
                    S.activation(cols[:, 16, 0:2 * Q], cols[:, 16, 0:2 * Q], ACT.Sqrt).then_inc(x1_std, 1)
                if step == 5:
                    act.wait_ge(v1_scale, g + 1)
                    wait_holder()
                    for i in range(Q):
                        ins = S.activation(v_sb[:, i, :], flat(x_sb[:, bass.ds(g * Q + i, 1), :]), ACT.Relu,
                                           scale=cols[:, 18, i:i + 1], bias=cols[:, 19, i:i + 1])
                    link(ins, base)
                    wait_holder()
                    S.activation(v_l1[:, bass.ds(g * Q, Q), 0:D], v_sb, ACT.Copy).then_inc(v1hi_ready, 1)
                    assert count[0] == LINKS

            def epilogue(g, par):
                for step in range(6):
                    epilogue_step(step, g, par)

            for g in range(FIRST):
                epilogue(g, 0)
            with act.Fori(FIRST // 2 + 1, PAIRS) as p:
                epilogue(p * 2 + (-1), 1)
                epilogue(p * 2, 0)

            def split_hi(p, k):
                act.wait_ge(slot_landed[k % RING], p * (PC // RING * 16) + 16 * ((CHUNKS - RING + k) // RING + 1))
                for h in range(2):
                    n0 = 2 * k + h
                    if isinstance(p, int) and n0 < BUF:
                        act.wait_ge(chunk_used, CHUNKS - RING + n0 // 2 + 1)
                    else:
                        act.wait_ge(half_used, p * (2 * PC) + (n0 - BUF + 1))
                    S.activation(hi[:, n0 % BUF, :], ring[:, k % RING, h * HALF:(h + 1) * HALF], ACT.Copy).then_inc(hi_ready, 1)

            def take_agg(g, par):
                act.wait_ge(half_used, g * (2 * CJ) + 2 * CJ)
                if not (isinstance(g, int) and g < 1):
                    act.wait_ge(lin_ready, g)
                S.activation(featT[:, par, :], num[:, par, :], ACT.Copy).then_inc(agg_ready, 1)

            def pair(p):
                first = isinstance(p, int)
                for k in range(PC):
                    split_hi(p, k)
                    if first and k % 2 == 1 and k < CJ - 4:
                        epilogue_step(k // 2, G - 1, 1)
                    if k == 2 and not first:
                        take_agg(p * 2 + (-1), 1)
                    if k == CJ + 2:
                        take_agg(p * 2, 0)

            pair(0)
            with act.Fori(1, PAIRS) as p:
                pair(p)
            take_agg(G - 1, 1)

        @block.vector
        def _(dve):
            count = [0]

            def link(ins, base=0):
                count[0] += 1
                ins.then_inc(dve_chain, 1)
                dve.wait_ge(dve_chain, base + count[0])

            V = nc.vector

            def artanh_before_ln(z, n, base):
                link(V.tensor_scalar(cols[:, 2, 0:n], z, -1.0, 1.0, ALU.mult, ALU.add), base)
                link(V.reciprocal(cols[:, 3, 0:n], cols[:, 2, 0:n]), base)
                return V.scalar_tensor_tensor(out=cols[:, 4, 0:n], in0=z, scalar=1.0, in1=cols[:, 3, 0:n],
                                              op0=ALU.add, op1=ALU.mult)

            def artanh_series(z, n, base):
                w, s = cols[:, 6, 0:n], cols[:, 7, 0:n]
                V.tensor_scalar(cols[:, 8, 0:n], z, 0.1, None, ALU.is_lt)
                link(V.tensor_tensor(w, z, z, ALU.mult), base)
                link(V.tensor_scalar(s, w, 1.0 / 9, None, ALU.mult), base)
                for c in (1.0 / 7, 1.0 / 5, 1.0 / 3):
                    link(V.scalar_tensor_tensor(out=s, in0=s, scalar=c, in1=w, op0=ALU.add, op1=ALU.mult), base)
                link(V.scalar_tensor_tensor(out=s, in0=s, scalar=1.0, in1=z, op0=ALU.add, op1=ALU.mult), base)

            def stats(b):
                t0, n = BATCHES[b]
                dve.wait_ge(x_landed[b], 16)
                for i in range(n):
                    ins = V.bn_stats(bn6[:, i, :], x_sb[:, t0 + i, :])
                link(ins)
                for i in range(n):
                    ins = V.bn_aggr(mv[:, b % 2, i, :], bn6[:, i, :])
                link(ins)
                V.tensor_scalar(rstd[:, b % 2, 0:n], mv[:, b % 2, 0:n, 1], LN_EPS, None, ALU.add).then_inc(var_ready, 1)

            def h_of(b):
                t0, n = BATCHES[b]
                dve.wait_ge(std_ready, b + 1)
                link(V.reciprocal(rstd[:, b % 2, 0:n], rstd[:, b % 2, 0:n]))
                for i in range(n):
                    ins = V.tensor_scalar(v_l0[:, t0 + i, 0:D], x_sb[:, t0 + i, :], mv[:, b % 2, i, 0:1],
                                          rstd[:, b % 2, i:i + 1], ALU.subtract, ALU.mult)
                link(ins)
                h = v_l0[:, t0:t0 + n, 0:D]
                V.tensor_scalar(h, h, 0.0, None, ALU.max).then_inc(h_ready, 1)

            def operand_begin(b):
                t0, n = BATCHES[b]
                dve.wait_ge(norms_ready, b + 1)
                norms = cols[:, 1, :]
                both = cols[:, 0:2, :].rearrange("p r (a n) -> p r a n", a=2)[:, :, :, 0:n]
                link(V.tensor_scalar(both[:, 1], both[:, 0], MIN_NORM, None, ALU.max))
                hn, mn = norms[:, 0:n], norms[:, MB:MB + n]
                z, w, rh, rm = cols[:, 10, 0:n], cols[:, 11, 0:n], cols[:, 14, 0:n], cols[:, 15, 0:n]
                link(V.tensor_scalar(z, hn, ONE, None, ALU.min))
                artanh_before_ln(z, n, 0).then_inc(ln_in, 1)
                artanh_series(z, n, 0)
                V.reciprocal(rm, mn)
                link(V.reciprocal(rh, hn))
                link(V.tensor_tensor(w, mn, rh, ALU.mult))
                dve.wait_ge(ln_out, b + 1)
                a = cols[:, 9, 0:n]
                link(V.tensor_scalar(a, cols[:, 5, 0:n], 0.5, None, ALU.mult))
                link(V.copy_predicated(a, cols[:, 8, 0:n].bitcast(U32), cols[:, 7, 0:n]))
                V.tensor_tensor(w, w, a, ALU.mult).then_inc(th_in, 1)

            def operand_end(b):
                t0, n = BATCHES[b]
                mn0, rm = cols[:, 0, MB:MB + n], cols[:, 15, 0:n]
                dve.wait_ge(th_out, b + 1)
                c, s, gm = cols[:, 13, 0:n], cols[:, 16, 0:n], cols[:, 17, 0:n]
                link(V.tensor_tensor(c, cols[:, 12, 0:n], rm, ALU.mult))
                link(V.tensor_tensor(s, c, mn0, ALU.mult))
                link(V.tensor_tensor(s, s, s, ALU.mult))
                link(V.tensor_scalar(s, s, -1.0, 1.0, ALU.mult, ALU.add))
                link(V.tensor_scalar(s, s, LN_EPS, None, ALU.max))
                link(V.reciprocal(gm, s))
                link(V.scalar_tensor_tensor(out=c, in0=gm, scalar=2.0, in1=c, op0=ALU.mult, op1=ALU.mult))
                V.tensor_scalar(v_l0[:, t0:t0 + n, D], gm, 2.0, -1.0, ALU.mult, ALU.add)
                for i in range(n):
                    v = v_l0[:, t0 + i, 0:D]
                    ins = V.tensor_scalar(v, v, cols[:, 13, i:i + 1], None, ALU.mult)
                ins.then_inc(v0_ready, 1)

            stats(0)
            h_of(0)
            stats(1)
            h_of(1)
            for b in range(NB):
                operand_begin(b)
                if 0 < b < NB - 2:
                    stats(b + 2)
                operand_end(b)
                if b == 0:
                    stats(2)
                if b + 2 < NB:
                    h_of(b + 2)
            dve.wait_ge(v0_ready, NB)
            V.memset(cols[:, 20, 2 * MB - 1:2 * MB], 0.0).then_inc(num_free, 1)

            chain0 = count[0]
            LINKS = 30

            def epilogue_step(step, g, par):
                n = Q
                base = g * LINKS + chain0
                den = cols[:, 20, 0:n]
                z, tn, inv, w, r = cols[:, 10, 0:n], cols[:, 1, 0:n], cols[:, 14, 0:n], cols[:, 11, 0:n], cols[:, 21, 0:n]
                if step == 0:
                    count[0] = 0
                    dve.wait_ge(chunk_used, max(g * CJ + CJ, FIRST_CHUNKS) if isinstance(g, int) else g * CJ + CJ)
                    ge, lt = cols[:, 15, 0:n], cols[:, 16, 0:n]
                    ins = V.tensor_copy(cols[:, 20:22, 0:n].rearrange("p c q -> p q c"), num[:, 4 * par:4 * par + 4, first_col(g) + D:first_col(g) + VW])
                    ins.then_inc(sums_taken, 1)
                    dve.wait_ge(sums_taken, g + 1)
                    V.tensor_scalar(ge, den, 0.0, None, ALU.is_ge)
                    link(V.tensor_scalar(lt, den, 0.0, None, ALU.is_lt), base)
                    V.scalar_tensor_tensor(out=ge, in0=den, scalar=1e-10, in1=ge, op0=ALU.max, op1=ALU.mult)
                    link(V.scalar_tensor_tensor(out=lt, in0=den, scalar=-1e-10, in1=lt, op0=ALU.min, op1=ALU.mult), base)
                    link(V.tensor_tensor(inv, ge, lt, ALU.add), base)
                    link(V.reciprocal(inv, inv), base)
                    link(V.scalar_tensor_tensor(out=tn, in0=inv, scalar=-1.0, in1=inv, op0=ALU.mult, op1=ALU.max), base)
                    dve.wait_ge(n_norm, g + 1)
                    link(V.tensor_tensor(tn, tn, cols[:, 0, 0:n], ALU.mult), base)
                    link(V.tensor_scalar(tn, tn, MIN_NORM, None, ALU.max), base)
                    link(V.tensor_scalar(z, tn, ONE, None, ALU.min), base)
                    artanh_before_ln(z, n, base).then_inc(e_ln_in, 1)
                if step == 1:
                    artanh_series(z, n, base)
                    link(V.reciprocal(tn, tn), base)
                    link(V.tensor_tensor(inv, inv, tn, ALU.mult), base)
                    dve.wait_ge(e_ln_out, g + 1)
                    a = cols[:, 9, 0:n]
                    link(V.tensor_scalar(a, cols[:, 5, 0:n], 0.5, None, ALU.mult), base)
                    V.tensor_scalar(w, r, 0.5, None, ALU.mult)
                    link(V.copy_predicated(a, cols[:, 8, 0:n].bitcast(U32), cols[:, 7, 0:n]), base)
                    link(V.tensor_tensor(w, w, a, ALU.mult), base)
                    link(V.tensor_scalar(w, w, CLIP, -CLIP, ALU.min, ALU.max), base)
                    V.tensor_tensor(cols[:, 13, 0:n], w, inv, ALU.mult).then_inc(u_scale, 1)
                if step == 2:
                    dve.wait_ge(u_norm, g + 1)
                    V.tensor_scalar(w, cols[:, 0, 0:n], MIN_NORM, None, ALU.max).then_inc(e_th_in, 1)
                if step == 3:
                    dve.wait_ge(e_th_in, g + 1)
                    link(V.reciprocal(cols[:, 15, 0:n], w), base)
                    dve.wait_ge(e_th_out, g + 1)
                    link(V.tensor_tensor(cols[:, 15, 0:n], cols[:, 15, 0:n], cols[:, 12, 0:n], ALU.mult), base)
                    for i in range(n):
                        xt = flat(x_sb[:, bass.ds(g * Q + i, 1), :])
                        ins = V.scalar_tensor_tensor(out=xt, in0=u_sb[:, i, :], scalar=cols[:, 15, i:i + 1], in1=xt, op0=ALU.mult, op1=ALU.add)
                    link(ins, base)
                    zero = cols[:, 15, 0:n]
                    V.tensor_scalar(zero, r, 0.0, None, ALU.is_equal)
                    for i in range(n):
                        ins = V.bn_stats(bn6[:, i, :], flat(x_sb[:, bass.ds(g * Q + i, 1), :]))
                    link(ins, base)
                    V.tensor_tensor(cols[:, 16, n:2 * n], r, zero, ALU.add)
                    for i in range(n):
                        ins = V.bn_aggr(mv[:, 0, i, :], bn6[:, i, :])
                    link(ins, base)
                    V.tensor_scalar(cols[:, 17, 0:n], zero, -1.0, 1.0, ALU.mult, ALU.add)
                    V.tensor_scalar(cols[:, 16, 0:n], mv[:, 0, 0:n, 1], LN_EPS, None, ALU.add).then_inc(x1_var, 1)
                if step == 4:
                    dve.wait_ge(x1_std, g + 1)
                    link(V.reciprocal(cols[:, 16, 0:2 * n], cols[:, 16, 0:2 * n]), base)
                    dt = dinv[:, bass.ds(g * Q, n)]
                    link(V.tensor_tensor(dt, cols[:, 16, n:2 * n], cols[:, 17, 0:n], ALU.mult), base)
                    link(V.tensor_tensor(cols[:, 18, 0:n], cols[:, 16, 0:n], dt, ALU.mult), base)
                    V.scalar_tensor_tensor(out=cols[:, 19, 0:n], in0=mv[:, 0, 0:n, 0], scalar=-1.0, in1=cols[:, 18, 0:n],
                                           op0=ALU.mult, op1=ALU.mult).then_inc(v1_scale, 1)
                    assert count[0] == LINKS, count
                if step == 5:
                    dve.wait_ge(v1hi_ready, g + 1)
                    vg = v_l1[:, bass.ds(g * Q, Q), :]
                    V.tensor_tensor(vg[:, :, D:2 * D], v_sb, vg[:, :, 0:D].bitcast(F32), ALU.subtract).then_inc(v1lo_ready, 1)

            def epilogue(g, par):
                for step in range(6):
                    epilogue_step(step, g, par)

            for g in range(FIRST):
                epilogue(g, 0)
            with dve.Fori(FIRST // 2 + 1, PAIRS) as p:
                epilogue(p * 2 + (-1), 1)
                epilogue(p * 2, 0)

            def split_lo(p, k):
                for h in range(2):
                    n0 = 2 * k + h
                    if isinstance(p, int) and n0 < BUF:
                        dve.wait_ge(chunk_used, last_reader((n0 + 1) * HALF * 4))
                    dve.wait_ge(hi_ready, p * (2 * PC) + (n0 + 1))
                    V.tensor_tensor(lo[:, n0 % BUF, :], ring[:, k % RING, h * HALF:(h + 1) * HALF],
                                    hi[:, n0 % BUF, :].bitcast(F32), ALU.subtract).then_inc(lo_ready, 1)

            def output(s, par):
                g = group_of(s)
                dve.wait_ge(lin_ready, s + 1)
                for q in range(Q):
                    xt = flat(x_sb[:, bass.ds(g * Q + q, 1), :])
                    ins = V.scalar_tensor_tensor(out=xt, in0=num[:, 2 + par, q * D:(q + 1) * D], scalar=dinv[:, bass.ds(g * Q + q, 1)],
                                                 in1=xt, op0=ALU.mult, op1=ALU.add)
                ins.then_inc(out_ready, 1)

            def pair(p):
                first = isinstance(p, int)
                for k in range(PC):
                    split_lo(p, k)
                    if first and k % 2 == 1 and k < CJ - 4:
                        epilogue_step(k // 2, G - 1, 1)
                    if first and k == CJ:
                        dve.wait_ge(x1b_ready, G)
                    if k == 4 and not first:
                        output(p * 2 + (-1), 1)
                    if k == CJ + 4:
                        output(p * 2, 0)

            pair(0)
            with dve.Fori(1, PAIRS) as p:
                pair(p)
            output(G - 1, 1)

        @block.tensor
        def _(pe):
            def transposes(q):
                b = [i for i, (t0, n) in enumerate(BATCHES) if t0 <= q * Q < t0 + n][0]
                pe.wait_ge(h_ready, b + 1)
                if q >= 2:
                    pe.wait_ge(hT_ready, q - 1)
                for i in range(Q):
                    ins = nc.tensor.transpose(num[:, 4 + q % 2, i * P:(i + 1) * P], v_l0[:, q * Q + i, 0:D], ident[:])
                ins.then_inc(hT_ps, 1)

            def products(q):
                pe.wait_ge(hT_ready, q + 1)
                if q >= 2:
                    pe.wait_ge(mx_moved, q - 1)
                for i in range(Q):
                    ins = nc.tensor.matmul(num[:, 6 + q % 2, i * D:(i + 1) * D], featT[:, q % 2, i * P:(i + 1) * P], w0_sb[:], start=True, stop=True)
                ins.then_inc(mx_ps, 1)

            def batch(b):
                t0, n = BATCHES[b]
                q0, q1 = t0 // Q, (t0 + n) // Q
                transposes(q0)
                for q in range(q0, q1):
                    if q + 1 < q1:
                        transposes(q + 1)
                    products(q)

            def chunk0(g, par, k):
                c0 = first_col(g)
                shared = isinstance(g, int) and g < FIRST - 1
                if isinstance(g, int) and g < FIRST:
                    c = k * FIRST + g
                    slot, quad = c % RING, k
                    pe.wait_ge(slot_landed[slot], 16 * (c // RING + 1))
                else:
                    slot, quad = k % RING, rotated(k)
                    pe.wait_ge(slot_landed[slot], g * (CJ // RING * 16) + 16 * (k // RING + 1))
                for jq in range(Q):
                    for q in range(Q):
                        at = slice((jq * Q + q) * P, (jq * Q + q + 1) * P)
                        ins = nc.tensor.matmul(num[:, 4 * par + q, c0:c0 + VW], ring[:, slot, at], v_l0[:, quad * Q + jq, :],
                                               start=k + jq + c0 == 0, stop=k == CJ - 1 and jq == Q - 1 and not shared)
                ins.then_inc(chunk_used, 1)

            def group0(g, par):
                if isinstance(g, int) and g == FIRST:
                    pe.wait_ge(num_free, 1)
                else:
                    pe.wait_ge(num_free, g)
                for k in range(CJ):
                    chunk0(g, par, k)

            pe.wait_ge(consts_landed, 64)
            batch(0)
            batch(1)
            pe.wait_ge(ones_set, 1)
            for b, (t0, n) in enumerate(BATCHES):
                pe.wait_ge(v0_ready, b + 1)
                for k in range(t0 // Q, (t0 + n) // Q):
                    for g in range(FIRST):
                        chunk0(g, 0, k)
                if b + 2 < NB:
                    batch(b + 2)
            group0(FIRST, 1)
            with pe.Fori(FIRST // 2 + 1, PAIRS) as p:
                group0(p * 2, 0)
                group0(p * 2 + 1, 1)

            def linear(g, par):
                pe.wait_ge(agg_ready, g + 1)
                if not (isinstance(g, int) and g < 1):
                    pe.wait_ge(out_ready, g)
                for q in range(Q):
                    ins = nc.tensor.matmul(num[:, 2 + par, q * D:(q + 1) * D], featT[:, par, q * P:(q + 1) * P], w1t_sb[:], start=True, stop=True)
                ins.then_inc(lin_ready, 1)

            def pair(p):
                first = isinstance(p, int)
                for par in range(2):
                    if first:
                        pe.wait_ge(num_free, G)
                    else:
                        pe.wait_ge(agg_ready, p * 2 + (par - 1))
                    for k in range(CJ):
                        if first and par == 0:
                            pe.wait_ge(v1lo_ready, k + 1)
                        acc = num[:, par, :]
                        for h in range(2):
                            n0 = 2 * (par * CJ + k) + h
                            pe.wait_ge(lo_ready, p * (2 * PC) + (n0 + 1))
                            for j in range(2):
                                v = v_l1[:, k * Q + 2 * h + j, :]
                                at = slice(j * Q * P, (j + 1) * Q * P)
                                nc.tensor.matmul(acc, v[:, 0:D], hi[:, n0 % BUF, at], start=k + h + j == 0, stop=False)
                                nc.tensor.matmul(acc, v[:, 0:D], lo[:, n0 % BUF, at], start=False, stop=False)
                                ins = nc.tensor.matmul(acc, v[:, D:2 * D], hi[:, n0 % BUF, at], start=False, stop=k == CJ - 1 and h + j == 2)
                            ins.then_inc(half_used, 1)
                        if k == 3 and not (first and par == 0):
                            linear(p * 2 + (par - 1), 1 - par)

            pair(0)
            with pe.Fori(1, PAIRS) as p:
                pair(p)
            linear(G - 1, 1)


def kernel(x, adj, L0_gnn_W, L1_gnn_W, L1_gnn_b):
    import concourse.bacc as _bacc
    from concourse.bass_utils import run_bass_kernel_spmd as _run

    a = np.asarray(adj).reshape(P, G, Q, P, CJ, Q).transpose(1, 4, 3, 5, 2, 0)
    arrays = {
        "x": np.ascontiguousarray(x),
        "adj": np.ascontiguousarray(a).reshape(CHUNKS * P, CHUNK),
        "W0": np.ascontiguousarray(L0_gnn_W),
        "W1T": np.ascontiguousarray(np.asarray(L1_gnn_W).T),
        "b1": np.ascontiguousarray(L1_gnn_b),
        "identity": np.eye(P, dtype=np.float32),
    }
    nc = _bacc.Bacc("TRN2", target_bir_lowering=False, num_devices=1)
    args = [nc.dram_tensor(n, v.shape, mybir.dt.from_np(v.dtype), kind="ExternalInput").ap() for n, v in arrays.items()]
    args.append(nc.dram_tensor("out", (N, D), F32, kind="ExternalOutput").ap())
    build_program(nc, *args)
    r = _run(nc, [arrays], core_ids=[0])
    return r.results[0]["out"]
```

```python
from contextlib import ExitStack

import numpy as np

import concourse.bass as bass
from concourse import mybir

F32 = mybir.dt.float32
F32R = mybir.dt.float32r
BF16 = mybir.dt.bfloat16
U32 = mybir.dt.uint32
ALU = mybir.AluOpType
ACT = mybir.ActivationFunctionType

P = 128
D = 128
NT = 64
N = P * NT
Q = 4
G = NT // Q
CJ = NT // Q
CHUNK = Q * Q * P
CHUNKS = G * CJ
LEVEL = 4
LEVELS = G // LEVEL
EARLIER = 8
EXTRA = 8
RING = 4
RING2 = 8
HALF = CHUNK // 2
BUF = 4
VW = D + 2
FIRST = 3
FIRST_CHUNKS = FIRST * CJ
BATCHES = [(0, 4), (4, 4), (8, 8), (16, 12), (28, 12), (40, 12), (52, 12)]
NB = len(BATCHES)
MB = 12
LN_EPS = 1e-5
MIN_NORM = 1e-15
LAST_STEPS = (1, 4, 6, 8, 10, 12)
ONE = float(np.float32(1.0 - 1e-5))
CLIP = float(np.arctanh(np.float64(ONE)))


def early_steps(l):
    return 6 if l < LEVELS - 1 else 4


def shared(l):
    return LEVEL * l


def alone(l):
    return CJ - shared(l)


def extra(l):
    return EXTRA if LEVEL * l >= EARLIER else 0


def sequence(l):
    seq = [(k, None) for k in range(alone(l))]
    for j in range(shared(l)):
        if j < extra(l):
            seq.append((None, shared(l - EARLIER // LEVEL) + j))
        seq.append((alone(l) + j, j))
    return seq


def rest(l):
    later = l + EARLIER // LEVEL
    return alone(l) - (extra(later) if later < LEVELS else 0)


def halves_before(l):
    return sum(LEVEL * 2 * (shared(i) + extra(i)) for i in range(l))


HALVES1 = halves_before(LEVELS)
LOADS1 = CHUNKS + EARLIER * EXTRA
PARTS = G - LEVEL + EARLIER


def half1(l, p, par):
    n = 2 * (shared(l) + extra(l))
    return p * (2 * n) + (halves_before(l) + (par - LEVEL * l) * n)


def loads_before(g):
    if isinstance(g, int) and g < EARLIER:
        return g * CJ
    return g * (CJ + EXTRA) + (-EXTRA * EARLIER)


def own_part(g):
    if isinstance(g, int) and g < EARLIER:
        return g - LEVEL
    return g * 2 + (-LEVEL - EARLIER + 1)


def own_part_before(g):
    return g - LEVEL - 1 if isinstance(g, int) and g <= EARLIER else g * 2 + (-LEVEL - EARLIER - 1)


def again(l, p, par, j):
    c = sum(LEVEL * rest(i) for i in range(l))
    return p * (2 * rest(l)) + (c + (par - LEVEL * l) * rest(l) + j)


def both_layers(l):
    return [(m, k, quad) for m, (k, quad) in enumerate(sequence(l)) if quad is not None]


def extra_end(l):
    return 2 * max(j + 1 for j, (m, k, quad) in enumerate(both_layers(l)) if k is None)


def own_bank(l, par):
    return 1 if extra(l) else par


def turns(p, l):
    if isinstance(p, int) and p == 0:
        return [(par, j) for j in range(rest(l)) for par in range(2)]
    return [(par, j) for par in range(2) for j in range(rest(l))]


def flat(ap):
    return ap.rearrange("p a b -> p (a b)")


def build_program(nc, x, adj, W0, W1T, b1, identity, out):
    with ExitStack() as ctx:
        def sb(name, shape, dt=F32):
            return ctx.enter_context(nc.sbuf_tensor(name, shape, dt))

        def sem(name):
            return ctx.enter_context(nc.semaphore(name))

        x_sb = sb("x_sb", [P, NT, D])
        v_l1 = sb("v_l1", [P, NT, 2 * D], F32R)
        ring = sb("ring", [P, RING, CHUNK])
        lo = sb("lo", [P, BUF, HALF], F32R)
        hi = sb("hi", [P, BUF, HALF], F32R)
        featT = sb("featT", [P, 2, Q * P])
        uv = sb("uv", [P, 2 * Q, D])
        u_sb, v_sb = uv[:, 0:Q, :], uv[:, Q:2 * Q, :]
        squares = uv[:].bitcast(BF16).rearrange("p a (b d) -> p (a b) d", b=2)
        held = sb("held", [P, 1])
        w0_sb = sb("w0_sb", [P, D])
        w1t_sb = sb("w1t_sb", [P, D])
        b_sb = sb("b_sb", [P, D])
        ident = sb("ident", [P, P])
        dinv = sb("dinv", [P, NT])
        bn6 = sb("bn6", [P, MB, 6])
        mv = sb("mv", [P, 2, MB, 2])
        rstd = sb("rstd", [P, 2, MB])
        sq2 = sb("sq2", [P, 2, 2, MB])
        cols = sb("cols", [P, 22, 2 * MB])
        with nc.sbuf_tensor("v_l0", [P, NT, VW], F32) as v_l0:
            pass
        low_slots = sb("low_slots", [P, 3, CHUNK])
        sb("between", [P, NT * VW - 4 * CHUNK])
        top_slot = sb("top_slot", [P, CHUNK])
        num = ctx.enter_context(nc.psum_tensor("num", [P, 8, 512], F32))

        x_landed = [sem(f"x_landed{b}") for b in range(NB)]
        consts_landed = sem("consts_landed")
        slot_landed = [sem(f"slot_landed{s}") for s in range(RING2)]
        chunk_used = sem("chunk_used")
        half_used = sem("half_used")
        hi_ready = sem("hi_ready")
        lo_ready = sem("lo_ready")
        num_free = sem("num_free")
        dve_chain = sem("dve_chain")
        act_chain = sem("act_chain")
        ones_set = sem("ones_set")
        var_ready = sem("var_ready")
        std_ready = sem("std_ready")
        h_ready = sem("h_ready")
        hT_ps = sem("hT_ps")
        hT_ready = sem("hT_ready")
        mx_ps = sem("mx_ps")
        mx_moved = sem("mx_moved")
        norms_ready = sem("norms_ready")
        ln_in = sem("ln_in")
        ln_out = sem("ln_out")
        th_in = sem("th_in")
        th_out = sem("th_out")
        v0_ready = sem("v0_ready")
        sums_taken = sem("sums_taken")
        n_norm = sem("n_norm")
        e_ln_in = sem("e_ln_in")
        e_ln_out = sem("e_ln_out")
        u_scale = sem("u_scale")
        u_norm = sem("u_norm")
        e_th_in = sem("e_th_in")
        e_th_out = sem("e_th_out")
        x1_var = sem("x1_var")
        x1_std = sem("x1_std")
        v1_scale = sem("v1_scale")
        v1hi_ready = sem("v1hi_ready")
        v1lo_ready = sem("v1lo_ready")
        x1b_ready = sem("x1b_ready")
        agg_ready = sem("agg_ready")
        lin_ready = sem("lin_ready")
        out_ready = sem("out_ready")
        stored = sem("stored")

        slots2 = [(top_slot[:], CHUNKS - 12), (low_slots[:, 0, :], CHUNKS - 8), (low_slots[:, 1, :], CHUNKS - 4),
                  (ring[:, 0, :], CHUNKS - 3), (ring[:, 1, :], CHUNKS - 2), (ring[:, 2, :], CHUNKS - 1), (ring[:, 3, :], CHUNKS),
                  (low_slots[:, 2, :], CHUNKS)]
        ring_at = [None, None, None, 0, 1, 2, 3, None]
        landed2 = [(7, 0), (4, 0), (5, 0)] + [(i, 16 * (LOADS1 // RING)) for i in range(RING)] + [(6, 0)]

        def bank_col(g, par, q):
            if isinstance(g, int) and g < FIRST:
                return q, g * VW
            return 6 - 2 * par + q // 2, q % 2 * VW

        x_dram = x.rearrange("(p t) d -> p t d", t=NT)
        out_dram = out.rearrange("(p t) d -> p t d", t=NT)
        block = ctx.enter_context(nc.Block())

        @block.sync
        def _(sp):
            for b, (t0, n) in enumerate(BATCHES):
                sp.dma_start(x_sb[:, t0:t0 + n, :], x_dram[:, t0:t0 + n, :]).then_inc(x_landed[b], 16)
                if b == 0:
                    for dst, src in ((ident, identity), (w0_sb, W0), (w1t_sb, W1T)):
                        sp.dma_start(dst[:], src).then_inc(consts_landed, 16)
                    sp.dma_start(b_sb[:], b1.rearrange("(o d) -> o d", o=1).to_broadcast([P, D])).then_inc(consts_landed, 16)

            def load(c, slot, landed):
                sp.dma_start(slot, adj[bass.ds(c * P, P), :]).then_inc(landed, 16)

            for c in range(FIRST_CHUNKS):
                if c >= RING:
                    sp.wait_ge(chunk_used, c - RING + 1)
                load(c % FIRST * CJ + c // FIRST, ring[:, c % RING, :], slot_landed[c % RING])

            def group(g, l, half0):
                seq = sequence(l)
                for m, (k, quad) in enumerate(seq):
                    halves = 2 * sum(q is not None for _, q in seq[:max(m - RING + 1, 0)])
                    if m < RING and not (isinstance(g, int) and g <= LEVEL):
                        sp.wait_ge(half_used, half0 + 2 * (m - RING + 1))
                    elif m >= RING and seq[m - RING][1] is not None:
                        sp.wait_ge(half_used, half0 + halves)
                    else:
                        sp.wait_ge(chunk_used, g * CJ + (m - RING + 1))
                    if k is None:
                        c = g * CJ + (quad - EARLIER * CJ)
                    else:
                        c = g * CJ + (k + shared(l)) % CJ
                    load(c, ring[:, m % RING, :], slot_landed[m % RING])

            group(FIRST, 0, 0)
            for g in range(LEVEL, 2 * LEVEL):
                group(g, 1, half1(1, g // 2, g % 2))
            for l in range(2, LEVELS):
                with sp.Fori(2 * l, 2 * l + 2) as p:
                    group(p * 2, l, half1(l, p, 0))
                    group(p * 2 + 1, l, half1(l, p, 1))

            def pair(p, l):
                for m, (par, j) in enumerate(turns(p, l)):
                    i = m % RING2
                    slot, free = slots2[i]
                    c = again(l, p, 0, 0) + m
                    if isinstance(c, int) and c < RING2:
                        sp.wait_ge(chunk_used, free)
                        if ring_at[i] is not None:
                            sp.wait_ge(lo_ready, HALVES1 - 2 * (RING - 1 - ring_at[i]))
                    else:
                        sp.wait_ge(lo_ready, c * 2 + (HALVES1 - 2 * (RING2 - 1)))
                    load(p * (2 * CJ) + (par * CJ + CJ - rest(l) + j), slot, slot_landed[landed2[i][0]])

            pair(0, 0)
            pair(1, 0)
            for l in range(1, LEVELS):
                with sp.Fori(2 * l, 2 * l + 2) as p:
                    pair(p, l)

        @block.gpsimd
        def _(pool):
            nc.gpsimd.memset(v_l0[:, :, D + 1:VW], 1.0).then_inc(ones_set, 1)
            pool.wait_ge(consts_landed, 64)

            with pool.Fori(0, G) as g:
                pool.wait_ge(v1hi_ready, g + 1)
                xs = x_sb[:, bass.ds(g * Q, Q), :]
                bias = b_sb[:].rearrange("p (o d) -> p o d", o=1).to_broadcast([P, Q, D])
                nc.gpsimd.tensor_tensor(xs, xs, bias, ALU.add).then_inc(x1b_ready, 1)

            with pool.Fori(0, G) as g:
                pool.wait_ge(out_ready, g + (PARTS + 1))
                pool.dma_start(out_dram[:, bass.ds(g * Q, Q), :], x_sb[:, bass.ds(g * Q, Q), :]).then_inc(stored, 16)
            pool.wait_ge(stored, 16 * G)

        @block.scalar
        def _(act):
            S = nc.scalar
            count = [0]

            def link(ins, base=0):
                count[0] += 1
                ins.then_inc(act_chain, 1)
                act.wait_ge(act_chain, base + count[0])

            def std(b):
                n = BATCHES[b][1]
                act.wait_ge(var_ready, b + 1)
                S.activation(rstd[:, b % 2, 0:n], rstd[:, b % 2, 0:n], ACT.Sqrt).then_inc(std_ready, 1)

            def h_norms(b):
                t0, n = BATCHES[b]
                act.wait_ge(h_ready, b + 1)
                for i in range(n):
                    ins = S.activation(squares[:, i, :], v_l0[:, t0 + i, 0:D], ACT.Square, accum_out=sq2[:, b % 2, 0, i:i + 1])
                link(ins)

            def move_quads(b):
                t0, n = BATCHES[b]
                q0, q1 = t0 // Q, (t0 + n) // Q
                for q in range(q0, q1 + 1):
                    if q < q1:
                        act.wait_ge(hT_ps, q + 1)
                        if q >= 2:
                            act.wait_ge(mx_ps, q - 1)
                        S.activation(featT[:, q % 2, :], num[:, 4 + q % 2, :], ACT.Copy).then_inc(hT_ready, 1)
                    if q > q0:
                        m = q - 1
                        act.wait_ge(mx_ps, m + 1)
                        S.activation(v_l0[:, m * Q:(m + 1) * Q, 0:D], num[:, 6 + m % 2, :].rearrange("p (a d) -> p a d", a=Q), ACT.Copy).then_inc(mx_moved, 1)

            def mx_norms(b):
                t0, n = BATCHES[b]
                act.wait_ge(mx_moved, (t0 + n) // Q)
                for i in range(n):
                    ins = S.activation(squares[:, i, :], v_l0[:, t0 + i, 0:D], ACT.Square, accum_out=sq2[:, b % 2, 1, i:i + 1])
                link(ins)
                if b >= 1:
                    act.wait_ge(v0_ready, b)
                both = cols[:, 0, :].rearrange("p (a n) -> p a n", a=2)[:, :, 0:n]
                S.activation(both, sq2[:, b % 2, :, 0:n], ACT.Sqrt).then_inc(norms_ready, 1)

            std(0)
            h_norms(0)
            std(1)
            move_quads(0)
            for b in range(NB):
                n = BATCHES[b][1]
                mx_norms(b)
                act.wait_ge(ln_in, b + 1)
                S.activation(cols[:, 5, 0:n], cols[:, 4, 0:n], ACT.Ln).then_inc(ln_out, 1)
                if b + 1 < NB:
                    h_norms(b + 1)
                act.wait_ge(th_in, b + 1)
                S.activation(cols[:, 12, 0:n], cols[:, 11, 0:n], ACT.Tanh).then_inc(th_out, 1)
                if b + 1 < NB:
                    move_quads(b + 1)
                if b + 2 < NB:
                    std(b + 2)

            chain0 = count[0]
            LINKS = 3

            def wait_holder():
                S.activation(held[:], cols[:, 13, 0:1], ACT.Copy)

            def epilogue_step(step, g, par):
                base = g * LINKS + chain0
                if step == 0:
                    count[0] = 0
                    if not (isinstance(g, int) and g < 1):
                        act.wait_ge(v1lo_ready, g)
                    act.wait_ge(sums_taken, g + 1)
                    for i in range(Q):
                        bank, c0 = bank_col(g, par, i)
                        ins = S.activation(squares[:, 2 * Q + i, :], num[:, bank, c0:c0 + D], ACT.Square, accum_out=sq2[:, 0, 0, i:i + 1])
                    link(ins, base)
                    S.activation(cols[:, 0, 0:Q], sq2[:, 0, 0, 0:Q], ACT.Sqrt).then_inc(n_norm, 1)
                if step == 1:
                    act.wait_ge(e_ln_in, g + 1)
                    S.activation(cols[:, 5, 0:Q], cols[:, 4, 0:Q], ACT.Ln).then_inc(e_ln_out, 1)
                if step == 2:
                    act.wait_ge(u_scale, g + 1)
                    for i in range(Q):
                        bank, c0 = bank_col(g, par, i)
                        ins = S.activation(u_sb[:, i, :], num[:, bank, c0:c0 + D], ACT.Relu, scale=cols[:, 13, i:i + 1])
                    ins.then_inc(num_free, 1)
                    act.wait_ge(num_free, g + 2)
                    for i in range(Q):
                        ins = S.activation(squares[:, 3 * Q + i, :], u_sb[:, i, :], ACT.Square, accum_out=sq2[:, 0, 1, i:i + 1])
                    link(ins, base)
                    S.activation(cols[:, 0, 0:Q], sq2[:, 0, 1, 0:Q], ACT.Sqrt).then_inc(u_norm, 1)
                if step == 3:
                    act.wait_ge(e_th_in, g + 1)
                    S.activation(cols[:, 12, 0:Q], cols[:, 11, 0:Q], ACT.Tanh).then_inc(e_th_out, 1)
                if step == 4:
                    act.wait_ge(x1_var, g + 1)
                    S.activation(cols[:, 16, 0:2 * Q], cols[:, 16, 0:2 * Q], ACT.Sqrt).then_inc(x1_std, 1)
                if step == 5:
                    act.wait_ge(v1_scale, g + 1)
                    wait_holder()
                    for i in range(Q):
                        ins = S.activation(v_sb[:, i, :], flat(x_sb[:, bass.ds(g * Q + i, 1), :]), ACT.Relu,
                                           scale=cols[:, 18, i:i + 1], bias=cols[:, 19, i:i + 1])
                    link(ins, base)
                    wait_holder()
                    S.activation(v_l1[:, bass.ds(g * Q, Q), 0:D], v_sb, ACT.Copy).then_inc(v1hi_ready, 1)
                    assert count[0] == LINKS

            def split_hi(slot, landed, value, half0, b0):
                act.wait_ge(landed, value)
                for h in range(2):
                    if not (isinstance(half0, int) and half0 + h < BUF):
                        act.wait_ge(half_used, half0 + (h - BUF + 1))
                    S.activation(hi[:, b0 + h, :], slot[:, h * HALF:(h + 1) * HALF], ACT.Copy).then_inc(hi_ready, 1)

            def take_agg(n, par, end):
                act.wait_ge(half_used, end)
                if not (isinstance(n, int) and n < 2):
                    act.wait_ge(lin_ready, n + (-1))
                S.activation(featT[:, par, :], num[:, par, :], ACT.Copy).then_inc(agg_ready, 1)

            def group(g, l, p, par):
                early = early_steps(l)
                if not (isinstance(g, int) and g <= LEVEL):
                    take_agg(own_part_before(g), own_bank(l, 1 - par), half1(l, p, par))
                for step in range(early):
                    epilogue_step(step, g + (-1), 1 - par)
                for j, (m, k, quad) in enumerate(both_layers(l)):
                    split_hi(ring[:, m % RING, :], slot_landed[m % RING], loads_before(g) * (16 // RING) + 16 * (m // RING + 1),
                             half1(l, p, par) + 2 * j, 2 * j % BUF)
                    if early + j < 6:
                        epilogue_step(early + j, g + (-1), 1 - par)
                if extra(l):
                    take_agg(own_part(g) + (-1), 0, half1(l, p, par) + extra_end(l))

            for g in range(FIRST):
                for step in range(6):
                    epilogue_step(step, g, 0)
            for g in range(LEVEL, 2 * LEVEL):
                group(g, 1, g // 2, g % 2)
            for l in range(2, LEVELS):
                with act.Fori(2 * l, 2 * l + 2) as p:
                    group(p * 2, l, p, 0)
                    group(p * 2 + 1, l, p, 1)

            def pair(p, l):
                first = isinstance(p, int) and p == 0
                for m, (par, j) in enumerate(turns(p, l)):
                    s, base = landed2[m % RING2]
                    value = again(l, p, 0, 0) * (16 // RING2) + (base + 16 * (m // RING2 + 1))
                    split_hi(slots2[m % RING2][0], slot_landed[s], value, again(l, p, 0, 0) * 2 + (HALVES1 + 2 * m), 2 * m % BUF)
                    if first:
                        if m == 0:
                            take_agg(PARTS - 1, 1, HALVES1)
                        if m in LAST_STEPS:
                            epilogue_step(LAST_STEPS.index(m), G - 1, 1)
                    elif isinstance(p, int) and p == 1 and m < 2:
                        take_agg(PARTS + m, m, again(l, p, 0, 0) * 2 + (HALVES1 - 2 + 2 * m))
                    elif j == 1:
                        take_agg(p * 2 + (PARTS - 1 + par), 1 - par, again(l, p, par, 0) * 2 + HALVES1)

            pair(0, 0)
            pair(1, 0)
            for l in range(1, LEVELS):
                with act.Fori(2 * l, 2 * l + 2) as p:
                    pair(p, l)
            take_agg(G + PARTS - 1, 1, 2 * CHUNKS)

        @block.vector
        def _(dve):
            count = [0]

            def link(ins, base=0):
                count[0] += 1
                ins.then_inc(dve_chain, 1)
                dve.wait_ge(dve_chain, base + count[0])

            V = nc.vector

            def artanh_before_ln(z, n, base):
                link(V.tensor_scalar(cols[:, 2, 0:n], z, -1.0, 1.0, ALU.mult, ALU.add), base)
                link(V.reciprocal(cols[:, 3, 0:n], cols[:, 2, 0:n]), base)
                return V.scalar_tensor_tensor(out=cols[:, 4, 0:n], in0=z, scalar=1.0, in1=cols[:, 3, 0:n],
                                              op0=ALU.add, op1=ALU.mult)

            def artanh_series(z, n, base):
                w, s = cols[:, 6, 0:n], cols[:, 7, 0:n]
                V.tensor_scalar(cols[:, 8, 0:n], z, 0.1, None, ALU.is_lt)
                link(V.tensor_tensor(w, z, z, ALU.mult), base)
                link(V.tensor_scalar(s, w, 1.0 / 9, None, ALU.mult), base)
                for c in (1.0 / 7, 1.0 / 5, 1.0 / 3):
                    link(V.scalar_tensor_tensor(out=s, in0=s, scalar=c, in1=w, op0=ALU.add, op1=ALU.mult), base)
                link(V.scalar_tensor_tensor(out=s, in0=s, scalar=1.0, in1=z, op0=ALU.add, op1=ALU.mult), base)

            def stats(b):
                t0, n = BATCHES[b]
                dve.wait_ge(x_landed[b], 16)
                for i in range(n):
                    ins = V.bn_stats(bn6[:, i, :], x_sb[:, t0 + i, :])
                link(ins)
                for i in range(n):
                    ins = V.bn_aggr(mv[:, b % 2, i, :], bn6[:, i, :])
                link(ins)
                V.tensor_scalar(rstd[:, b % 2, 0:n], mv[:, b % 2, 0:n, 1], LN_EPS, None, ALU.add).then_inc(var_ready, 1)

            def h_of(b):
                t0, n = BATCHES[b]
                dve.wait_ge(std_ready, b + 1)
                link(V.reciprocal(rstd[:, b % 2, 0:n], rstd[:, b % 2, 0:n]))
                for i in range(n):
                    ins = V.tensor_scalar(v_l0[:, t0 + i, 0:D], x_sb[:, t0 + i, :], mv[:, b % 2, i, 0:1],
                                          rstd[:, b % 2, i:i + 1], ALU.subtract, ALU.mult)
                link(ins)
                h = v_l0[:, t0:t0 + n, 0:D]
                V.tensor_scalar(h, h, 0.0, None, ALU.max).then_inc(h_ready, 1)

            def operand_begin(b):
                t0, n = BATCHES[b]
                dve.wait_ge(norms_ready, b + 1)
                norms = cols[:, 1, :]
                both = cols[:, 0:2, :].rearrange("p r (a n) -> p r a n", a=2)[:, :, :, 0:n]
                link(V.tensor_scalar(both[:, 1], both[:, 0], MIN_NORM, None, ALU.max))
                hn, mn = norms[:, 0:n], norms[:, MB:MB + n]
                z, w, rh, rm = cols[:, 10, 0:n], cols[:, 11, 0:n], cols[:, 14, 0:n], cols[:, 15, 0:n]
                link(V.tensor_scalar(z, hn, ONE, None, ALU.min))
                artanh_before_ln(z, n, 0).then_inc(ln_in, 1)
                artanh_series(z, n, 0)
                V.reciprocal(rm, mn)
                link(V.reciprocal(rh, hn))
                link(V.tensor_tensor(w, mn, rh, ALU.mult))
                dve.wait_ge(ln_out, b + 1)
                a = cols[:, 9, 0:n]
                link(V.tensor_scalar(a, cols[:, 5, 0:n], 0.5, None, ALU.mult))
                link(V.copy_predicated(a, cols[:, 8, 0:n].bitcast(U32), cols[:, 7, 0:n]))
                V.tensor_tensor(w, w, a, ALU.mult).then_inc(th_in, 1)

            def operand_end(b):
                t0, n = BATCHES[b]
                mn0, rm = cols[:, 0, MB:MB + n], cols[:, 15, 0:n]
                dve.wait_ge(th_out, b + 1)
                c, s, gm = cols[:, 13, 0:n], cols[:, 16, 0:n], cols[:, 17, 0:n]
                link(V.tensor_tensor(c, cols[:, 12, 0:n], rm, ALU.mult))
                link(V.tensor_tensor(s, c, mn0, ALU.mult))
                link(V.tensor_tensor(s, s, s, ALU.mult))
                link(V.tensor_scalar(s, s, -1.0, 1.0, ALU.mult, ALU.add))
                link(V.tensor_scalar(s, s, LN_EPS, None, ALU.max))
                link(V.reciprocal(gm, s))
                link(V.scalar_tensor_tensor(out=c, in0=gm, scalar=2.0, in1=c, op0=ALU.mult, op1=ALU.mult))
                V.tensor_scalar(v_l0[:, t0:t0 + n, D], gm, 2.0, -1.0, ALU.mult, ALU.add)
                for i in range(n):
                    v = v_l0[:, t0 + i, 0:D]
                    ins = V.tensor_scalar(v, v, cols[:, 13, i:i + 1], None, ALU.mult)
                ins.then_inc(v0_ready, 1)

            stats(0)
            h_of(0)
            stats(1)
            h_of(1)
            for b in range(NB):
                operand_begin(b)
                if 0 < b < NB - 2:
                    stats(b + 2)
                operand_end(b)
                if b == 0:
                    stats(2)
                if b + 2 < NB:
                    h_of(b + 2)
            dve.wait_ge(v0_ready, NB)
            V.memset(cols[:, 20, 2 * MB - 1:2 * MB], 0.0).then_inc(num_free, 1)

            chain0 = count[0]
            LINKS = 30

            def epilogue_step(step, g, par):
                n = Q
                base = g * LINKS + chain0
                den = cols[:, 20, 0:n]
                z, tn, inv, w, r = cols[:, 10, 0:n], cols[:, 1, 0:n], cols[:, 14, 0:n], cols[:, 11, 0:n], cols[:, 21, 0:n]
                if step == 0:
                    count[0] = 0
                    dve.wait_ge(chunk_used, max(g * CJ + CJ, FIRST_CHUNKS) if isinstance(g, int) else g * CJ + CJ)
                    ge, lt = cols[:, 15, 0:n], cols[:, 16, 0:n]
                    bank, c0 = bank_col(g, par, 0)
                    if isinstance(g, int) and g < FIRST:
                        ins = V.tensor_copy(cols[:, 20:22, 0:n].rearrange("p c q -> p q c"), num[:, 0:4, c0 + D:c0 + VW])
                    else:
                        ins = V.tensor_copy(cols[:, 20:22, 0:n].rearrange("p c (b h) -> p b h c", b=2),
                                            num[:, bank:bank + 2, 0:2 * VW].rearrange("p b (h c) -> p b h c", h=2)[:, :, :, D:VW])
                    ins.then_inc(sums_taken, 1)
                    dve.wait_ge(sums_taken, g + 1)
                    V.tensor_scalar(ge, den, 0.0, None, ALU.is_ge)
                    link(V.tensor_scalar(lt, den, 0.0, None, ALU.is_lt), base)
                    V.scalar_tensor_tensor(out=ge, in0=den, scalar=1e-10, in1=ge, op0=ALU.max, op1=ALU.mult)
                    link(V.scalar_tensor_tensor(out=lt, in0=den, scalar=-1e-10, in1=lt, op0=ALU.min, op1=ALU.mult), base)
                    link(V.tensor_tensor(inv, ge, lt, ALU.add), base)
                    link(V.reciprocal(inv, inv), base)
                    link(V.scalar_tensor_tensor(out=tn, in0=inv, scalar=-1.0, in1=inv, op0=ALU.mult, op1=ALU.max), base)
                    dve.wait_ge(n_norm, g + 1)
                    link(V.tensor_tensor(tn, tn, cols[:, 0, 0:n], ALU.mult), base)
                    link(V.tensor_scalar(tn, tn, MIN_NORM, None, ALU.max), base)
                    link(V.tensor_scalar(z, tn, ONE, None, ALU.min), base)
                    artanh_before_ln(z, n, base).then_inc(e_ln_in, 1)
                if step == 1:
                    artanh_series(z, n, base)
                    link(V.reciprocal(tn, tn), base)
                    link(V.tensor_tensor(inv, inv, tn, ALU.mult), base)
                    dve.wait_ge(e_ln_out, g + 1)
                    a = cols[:, 9, 0:n]
                    link(V.tensor_scalar(a, cols[:, 5, 0:n], 0.5, None, ALU.mult), base)
                    V.tensor_scalar(w, r, 0.5, None, ALU.mult)
                    link(V.copy_predicated(a, cols[:, 8, 0:n].bitcast(U32), cols[:, 7, 0:n]), base)
                    link(V.tensor_tensor(w, w, a, ALU.mult), base)
                    link(V.tensor_scalar(w, w, CLIP, -CLIP, ALU.min, ALU.max), base)
                    V.tensor_tensor(cols[:, 13, 0:n], w, inv, ALU.mult).then_inc(u_scale, 1)
                if step == 2:
                    dve.wait_ge(u_norm, g + 1)
                    V.tensor_scalar(w, cols[:, 0, 0:n], MIN_NORM, None, ALU.max).then_inc(e_th_in, 1)
                if step == 3:
                    dve.wait_ge(e_th_in, g + 1)
                    link(V.reciprocal(cols[:, 15, 0:n], w), base)
                    dve.wait_ge(e_th_out, g + 1)
                    link(V.tensor_tensor(cols[:, 15, 0:n], cols[:, 15, 0:n], cols[:, 12, 0:n], ALU.mult), base)
                    for i in range(n):
                        xt = flat(x_sb[:, bass.ds(g * Q + i, 1), :])
                        ins = V.scalar_tensor_tensor(out=xt, in0=u_sb[:, i, :], scalar=cols[:, 15, i:i + 1], in1=xt, op0=ALU.mult, op1=ALU.add)
                    link(ins, base)
                    zero = cols[:, 15, 0:n]
                    V.tensor_scalar(zero, r, 0.0, None, ALU.is_equal)
                    for i in range(n):
                        ins = V.bn_stats(bn6[:, i, :], flat(x_sb[:, bass.ds(g * Q + i, 1), :]))
                    link(ins, base)
                    V.tensor_tensor(cols[:, 16, n:2 * n], r, zero, ALU.add)
                    for i in range(n):
                        ins = V.bn_aggr(mv[:, 0, i, :], bn6[:, i, :])
                    link(ins, base)
                    V.tensor_scalar(cols[:, 17, 0:n], zero, -1.0, 1.0, ALU.mult, ALU.add)
                    V.tensor_scalar(cols[:, 16, 0:n], mv[:, 0, 0:n, 1], LN_EPS, None, ALU.add).then_inc(x1_var, 1)
                if step == 4:
                    dve.wait_ge(x1_std, g + 1)
                    link(V.reciprocal(cols[:, 16, 0:2 * n], cols[:, 16, 0:2 * n]), base)
                    dt = dinv[:, bass.ds(g * Q, n)]
                    link(V.tensor_tensor(dt, cols[:, 16, n:2 * n], cols[:, 17, 0:n], ALU.mult), base)
                    link(V.tensor_tensor(cols[:, 18, 0:n], cols[:, 16, 0:n], dt, ALU.mult), base)
                    V.scalar_tensor_tensor(out=cols[:, 19, 0:n], in0=mv[:, 0, 0:n, 0], scalar=-1.0, in1=cols[:, 18, 0:n],
                                           op0=ALU.mult, op1=ALU.mult).then_inc(v1_scale, 1)
                    assert count[0] == LINKS, count
                if step == 5:
                    dve.wait_ge(v1hi_ready, g + 1)
                    vg = v_l1[:, bass.ds(g * Q, Q), :]
                    V.tensor_tensor(vg[:, :, D:2 * D], v_sb, vg[:, :, 0:D].bitcast(F32), ALU.subtract).then_inc(v1lo_ready, 1)

            def split_lo(slot, half0, b0):
                for h in range(2):
                    dve.wait_ge(hi_ready, half0 + (h + 1))
                    V.tensor_tensor(lo[:, b0 + h, :], slot[:, h * HALF:(h + 1) * HALF],
                                    hi[:, b0 + h, :].bitcast(F32), ALU.subtract).then_inc(lo_ready, 1)

            def output(n, g, par):
                dve.wait_ge(lin_ready, n + 1)
                for q in range(Q):
                    xt = flat(x_sb[:, bass.ds(g * Q + q, 1), :])
                    ins = V.scalar_tensor_tensor(out=xt, in0=num[:, 2 + par, q * D:(q + 1) * D], scalar=dinv[:, bass.ds(g * Q + q, 1)],
                                                 in1=xt, op0=ALU.mult, op1=ALU.add)
                ins.then_inc(out_ready, 1)

            def group(g, l, p, par):
                early = early_steps(l)
                for step in range(early):
                    epilogue_step(step, g + (-1), 1 - par)
                for j, (m, k, quad) in enumerate(both_layers(l)):
                    split_lo(ring[:, m % RING, :], half1(l, p, par) + 2 * j, 2 * j % BUF)
                    if early + j < 6:
                        epilogue_step(early + j, g + (-1), 1 - par)
                    if j == 3 and not (isinstance(g, int) and g <= LEVEL):
                        dve.wait_ge(x1b_ready, g)
                        output(own_part_before(g), g + (-1), own_bank(l, 1 - par))
                if extra(l):
                    output(own_part(g) + (-1), g + (-EARLIER), 0)

            for g in range(FIRST):
                for step in range(6):
                    epilogue_step(step, g, 0)
            for g in range(LEVEL, 2 * LEVEL):
                group(g, 1, g // 2, g % 2)
            for l in range(2, LEVELS):
                with dve.Fori(2 * l, 2 * l + 2) as p:
                    group(p * 2, l, p, 0)
                    group(p * 2 + 1, l, p, 1)

            def pair(p, l):
                first = isinstance(p, int) and p == 0
                for m, (par, j) in enumerate(turns(p, l)):
                    split_lo(slots2[m % RING2][0], again(l, p, 0, 0) * 2 + (HALVES1 + 2 * m), 2 * m % BUF)
                    if first:
                        if m in LAST_STEPS:
                            epilogue_step(LAST_STEPS.index(m), G - 1, 1)
                        if m == 13:
                            dve.wait_ge(x1b_ready, G)
                            output(PARTS - 1, G - 1, 1)
                    elif isinstance(p, int) and p == 1 and m < 4:
                        if m % 2 == 1:
                            output(PARTS + m // 2, m // 2, m // 2)
                    elif j == 3:
                        output(p * 2 + (PARTS - 1 + par), p * 2 + (par - 1), 1 - par)

            pair(0, 0)
            pair(1, 0)
            for l in range(1, LEVELS):
                with dve.Fori(2 * l, 2 * l + 2) as p:
                    pair(p, l)
            output(G + PARTS - 1, G - 1, 1)

        @block.tensor
        def _(pe):
            def transposes(q):
                b = [i for i, (t0, n) in enumerate(BATCHES) if t0 <= q * Q < t0 + n][0]
                pe.wait_ge(h_ready, b + 1)
                if q >= 2:
                    pe.wait_ge(hT_ready, q - 1)
                for i in range(Q):
                    ins = nc.tensor.transpose(num[:, 4 + q % 2, i * P:(i + 1) * P], v_l0[:, q * Q + i, 0:D], ident[:])
                ins.then_inc(hT_ps, 1)

            def products(q):
                pe.wait_ge(hT_ready, q + 1)
                if q >= 2:
                    pe.wait_ge(mx_moved, q - 1)
                for i in range(Q):
                    ins = nc.tensor.matmul(num[:, 6 + q % 2, i * D:(i + 1) * D], featT[:, q % 2, i * P:(i + 1) * P], w0_sb[:], start=True, stop=True)
                ins.then_inc(mx_ps, 1)

            def batch(b):
                t0, n = BATCHES[b]
                q0, q1 = t0 // Q, (t0 + n) // Q
                transposes(q0)
                for q in range(q0, q1):
                    if q + 1 < q1:
                        transposes(q + 1)
                    products(q)

            def chunk0(g, par, k, l=0, m=0):
                if isinstance(g, int) and g < FIRST:
                    c = k * FIRST + g
                    slot, quad = c % RING, k
                    pe.wait_ge(slot_landed[slot], 16 * (c // RING + 1))
                    opens, closes = [g == 0] * Q, [g == FIRST - 1] * Q
                else:
                    slot, quad = m % RING, (k + shared(l)) % CJ
                    pe.wait_ge(slot_landed[slot], loads_before(g) * (16 // RING) + 16 * (m // RING + 1))
                    opens, closes = [True, False] * 2, [False, True] * 2
                for jq in range(Q):
                    for q in range(Q):
                        at = slice((jq * Q + q) * P, (jq * Q + q + 1) * P)
                        bank, c0 = bank_col(g, par, q)
                        ins = nc.tensor.matmul(num[:, bank, c0:c0 + VW], ring[:, slot, at], v_l0[:, quad * Q + jq, :],
                                               start=k + jq == 0 and opens[q], stop=k == CJ - 1 and jq == Q - 1 and closes[q])
                ins.then_inc(chunk_used, 1)

            def chunk1(half0, b0, quad, par, opens, closes):
                acc = num[:, par, :]
                for h in range(2):
                    pe.wait_ge(lo_ready, half0 + (h + 1))
                    for j in range(2):
                        v = v_l1[:, quad * Q + 2 * h + j, :]
                        at = slice(j * Q * P, (j + 1) * Q * P)
                        nc.tensor.matmul(acc, v[:, 0:D], hi[:, b0 + h, at], start=opens and h + j == 0, stop=False)
                        nc.tensor.matmul(acc, v[:, 0:D], lo[:, b0 + h, at], start=False, stop=False)
                        ins = nc.tensor.matmul(acc, v[:, D:2 * D], hi[:, b0 + h, at], start=False, stop=closes and h + j == 2)
                    ins.then_inc(half_used, 1)

            def linear(n, par):
                pe.wait_ge(agg_ready, n + 1)
                if not (isinstance(n, int) and n < 2):
                    pe.wait_ge(out_ready, n + (-1))
                for q in range(Q):
                    ins = nc.tensor.matmul(num[:, 2 + par, q * D:(q + 1) * D], featT[:, par, q * P:(q + 1) * P], w1t_sb[:], start=True, stop=True)
                ins.then_inc(lin_ready, 1)

            def group(g, par, l, p):
                pe.wait_ge(num_free, 1 if isinstance(g, int) and g == FIRST else g)
                both = both_layers(l)
                for m, (k, quad) in enumerate(sequence(l)):
                    if k is not None:
                        chunk0(g, par, k, l, m)
                    if m == 2 and not (isinstance(g, int) and g <= LEVEL):
                        linear(own_part_before(g), own_bank(l, 1 - par))
                    if quad is not None:
                        pe.wait_ge(v1lo_ready, quad + 1)
                        j = both.index((m, k, quad))
                        kind = [b for b in both if (b[1] is None) == (k is None)]
                        bank = 0 if k is None else own_bank(l, par)
                        chunk1(half1(l, p, par) + 2 * j, 2 * j % BUF, quad, bank, kind[0][0] == m, kind[-1][0] == m)
                if extra(l):
                    linear(own_part(g) + (-1), 0)

            pe.wait_ge(consts_landed, 64)
            batch(0)
            batch(1)
            pe.wait_ge(ones_set, 1)
            for b, (t0, n) in enumerate(BATCHES):
                pe.wait_ge(v0_ready, b + 1)
                for k in range(t0 // Q, (t0 + n) // Q):
                    for g in range(FIRST):
                        chunk0(g, 0, k)
                if b + 2 < NB:
                    batch(b + 2)
            group(FIRST, 1, 0, 0)
            for g in range(LEVEL, 2 * LEVEL):
                group(g, g % 2, 1, g // 2)
            for l in range(2, LEVELS):
                with pe.Fori(2 * l, 2 * l + 2) as p:
                    group(p * 2, 0, l, p)
                    group(p * 2 + 1, 1, l, p)

            def pair(p, l):
                first = isinstance(p, int) and p == 0
                for m, (par, j) in enumerate(turns(p, l)):
                    if j == 0:
                        pe.wait_ge(agg_ready, p * 2 + (PARTS - 1 + par))
                    if first and par == 0:
                        pe.wait_ge(v1lo_ready, CJ - rest(l) + j + 1)
                    chunk1(again(l, p, 0, 0) * 2 + (HALVES1 + 2 * m), 2 * m % BUF, CJ - rest(l) + j, par, j == 0, j == rest(l) - 1)
                    if first:
                        if m == 4:
                            linear(PARTS - 1, 1)
                    elif isinstance(p, int) and p == 1 and m < 3:
                        if m != 1:
                            linear(PARTS + m // 2, m // 2)
                    elif j == 2:
                        linear(p * 2 + (PARTS - 1 + par), 1 - par)

            pair(0, 0)
            pair(1, 0)
            for l in range(1, LEVELS):
                with pe.Fori(2 * l, 2 * l + 2) as p:
                    pair(p, l)
            linear(G + PARTS - 1, 1)


def kernel(x, adj, L0_gnn_W, L1_gnn_W, L1_gnn_b):
    import concourse.bacc as _bacc
    from concourse.bass_utils import run_bass_kernel_spmd as _run

    a = np.asarray(adj).reshape(P, G, Q, P, CJ, Q).transpose(1, 4, 3, 5, 2, 0)
    arrays = {
        "x": np.ascontiguousarray(x),
        "adj": np.ascontiguousarray(a).reshape(CHUNKS * P, CHUNK),
        "W0": np.ascontiguousarray(L0_gnn_W),
        "W1T": np.ascontiguousarray(np.asarray(L1_gnn_W).T),
        "b1": np.ascontiguousarray(L1_gnn_b),
        "identity": np.eye(P, dtype=np.float32),
    }
    nc = _bacc.Bacc("TRN2", target_bir_lowering=False, num_devices=1)
    args = [nc.dram_tensor(n, v.shape, mybir.dt.from_np(v.dtype), kind="ExternalInput").ap() for n, v in arrays.items()]
    args.append(nc.dram_tensor("out", (N, D), F32, kind="ExternalOutput").ap())
    build_program(nc, *args)
    r = _run(nc, [arrays], core_ids=[0])
    return r.results[0]["out"]
```
